# Optimizing a Trainium2 kernel written in Bass

```python
import numpy as np
import jax
import jax.numpy as jnp

def _softmax(x, axis=-1):
    return jax.nn.softmax(x, axis=axis)

def _gelu(x):
    return jax.nn.gelu(x, approximate=True)

def _silu(x):
    return jax.nn.silu(x)

def _sigmoid(x):
    return jax.nn.sigmoid(x)

def _layernorm(x, axis=-1, eps=1e-05):
    m = jnp.mean(x, axis=axis, keepdims=True)
    v = jnp.var(x, axis=axis, keepdims=True)
    return (x - m) / jnp.sqrt(v + eps)

def _scatter_add(tgt, idx, src, axis=0):
    return tgt.at[idx].add(src)

def _segment_sum(src, seg, n):
    return jax.ops.segment_sum(src, seg, n)
kernel_name = 'mk_gnn_preln_d2_gnn_r8_c65a3f'

def setup_inputs(seed: int=0):
    np.random.seed(seed)
    _w = jnp.asarray

    def _rec_inputs():
        import jax
        import jax.numpy as jnp
        _gk = jax.random.key(seed)
        x = -0.000202 + 1 * jax.random.normal(jax.random.fold_in(_gk, 1), (12500, 128), jnp.float32)
        _s = jax.random.randint(jax.random.fold_in(_gk, 2), (100000,), 0, 12500, jnp.int32)
        _d = jax.random.randint(jax.random.fold_in(_gk, 3), (100000,), 0, 12500, jnp.int32)
        _loop = jnp.arange(12500, dtype=jnp.int32)
        src = jnp.concatenate([_s, _d, _loop])
        dst = jnp.concatenate([_d, _s, _loop])
        _o = jnp.argsort(dst, stable=True)
        src = src[_o]
        dst = dst[_o]
        edge_attr_128 = -5.16925e-05 + 1.00005 * jax.random.normal(jax.random.fold_in(_gk, 11), (212500, 128), jnp.float32)
        return (x, src, dst, edge_attr_128)
    x, src, dst, edge_attr_128 = _rec_inputs()

    def _L0_gnn_setup():
        import jax, jax.numpy as jnp
        import numpy as np
        N_NODES = 6250
        N_EDGES = 200000
        IN_F = 128
        HEADS = 4
        HEAD_DIM = 32
        NEG_SLOPE = 0.2
        key = jax.random.key(seed)
        k1, k2, k3, k4 = jax.random.split(key, 4)
        x = jax.random.normal(k1, (N_NODES, IN_F), dtype=jnp.float32)
        edge_index = jax.random.randint(k2, (2, N_EDGES), 0, N_NODES, dtype=jnp.int64)
        W = jax.random.normal(k3, (HEADS * HEAD_DIM, IN_F), dtype=jnp.float32) * (1.0 / np.sqrt(IN_F))
        a = jax.random.normal(k4, (HEADS, 2 * HEAD_DIM), dtype=jnp.float32) * (1.0 / np.sqrt(2 * HEAD_DIM))
        return {'x': x, 'edge_index': edge_index, 'W': W, 'a': a}
    _L0_gnn_all = _L0_gnn_setup()
    _L0_gnn_in = {k: v for k, v in _L0_gnn_all.items() if k in ('W', 'a')}
    del _L0_gnn_all

    def _L1_gnn_setup():
        import jax, jax.numpy as jnp
        import numpy as np
        N_NODES = 6250
        N_EDGES = 100000
        HIDDEN = 128
        key = jax.random.key(seed)
        ks = jax.random.split(key, 6)
        h = jax.random.normal(ks[0], (N_NODES, HIDDEN), dtype=jnp.float32)
        edge_indices = jax.random.randint(ks[1], (2, N_EDGES), 0, N_NODES, dtype=jnp.int64)
        edge_attr = jax.random.normal(ks[2], (N_EDGES, HIDDEN), dtype=jnp.float32)
        scale = 1.0 / np.sqrt(3 * HIDDEN)
        W_weight = jax.random.normal(ks[3], (3 * HIDDEN, HIDDEN), dtype=jnp.float32) * scale
        b_weight = jnp.zeros((HIDDEN,), dtype=jnp.float32)
        W_gate = jax.random.normal(ks[4], (3 * HIDDEN, HIDDEN), dtype=jnp.float32) * scale
        b_gate = jnp.zeros((HIDDEN,), dtype=jnp.float32)
        return {'h': h, 'edge_indices': edge_indices, 'edge_attr': edge_attr, 'W_weight': W_weight, 'b_weight': b_weight, 'W_gate': W_gate, 'b_gate': b_gate}
    _L1_gnn_all = _L1_gnn_setup()
    _L1_gnn_in = {k: v for k, v in _L1_gnn_all.items() if k in ('W_weight', 'b_weight', 'W_gate', 'b_gate')}
    del _L1_gnn_all
    return {'x': x, 'src': src, 'dst': dst, 'edge_attr_128': edge_attr_128, 'L0_gnn_W': _L0_gnn_in['W'], 'L0_gnn_a': _L0_gnn_in['a'], 'L1_gnn_W_weight': _L1_gnn_in['W_weight'], 'L1_gnn_b_weight': _L1_gnn_in['b_weight'], 'L1_gnn_W_gate': _L1_gnn_in['W_gate'], 'L1_gnn_b_gate': _L1_gnn_in['b_gate']}

def reference(x, src, dst, edge_attr_128, L0_gnn_W, L0_gnn_a, L1_gnn_W_weight, L1_gnn_b_weight, L1_gnn_W_gate, L1_gnn_b_gate):
    import jax
    import jax.numpy as jnp

    def _L0_gnn_ref(x, edge_index, W, a):
        import jax, jax.numpy as jnp
        import numpy as np
        N_NODES = 6250
        N_EDGES = 200000
        IN_F = 128
        HEADS = 4
        HEAD_DIM = 32
        NEG_SLOPE = 0.2
        N = x.shape[0]
        h = (x @ W.T).reshape(N, HEADS, HEAD_DIM)
        src, dst = (edge_index[0], edge_index[1])
        a_src = a[:, :HEAD_DIM]
        a_dst = a[:, HEAD_DIM:]
        h_src = h[src]
        h_dst = h[dst]
        att = jnp.einsum('ehd,hd->eh', h_src, a_src) + jnp.einsum('ehd,hd->eh', h_dst, a_dst)
        att = jax.nn.leaky_relu(att, negative_slope=NEG_SLOPE)
        msgs = att[..., None] * h_src
        out = jax.ops.segment_sum(msgs, dst, num_segments=N)
        return out.reshape(N, HEADS * HEAD_DIM)

    def _L1_gnn_ref(h, edge_indices, edge_attr, W_weight, b_weight, W_gate, b_gate):
        import jax, jax.numpy as jnp
        import numpy as np
        N_NODES = 6250
        N_EDGES = 100000
        HIDDEN = 128
        row = edge_indices[0]
        col = edge_indices[1]
        edge_input = jnp.concatenate([h[row], h[col], edge_attr], axis=-1)
        messages = jax.nn.relu(edge_input @ W_weight + b_weight)
        gates = jax.nn.sigmoid(edge_input @ W_gate + b_gate)
        messages = messages * gates
        h_new = jax.ops.segment_sum(messages, row, num_segments=h.shape[0])
        return h_new
    edge_index = jnp.stack([src, dst])
    h = jnp.maximum(_layernorm(x, axis=-1), 0.0)
    x = x + _L0_gnn_ref(h, edge_index, L0_gnn_W, L0_gnn_a)
    h = jnp.maximum(_layernorm(x, axis=-1), 0.0)
    x = x + _L1_gnn_ref(h, edge_index, edge_attr_128, L1_gnn_W_weight, L1_gnn_b_weight, L1_gnn_W_gate, L1_gnn_b_gate)
    return x

_drawn_inputs = setup_inputs


def setup_inputs(seed=0):
    import zlib

    import numpy as np

    out = dict(_drawn_inputs(seed))
    spreads = {'L1_gnn_b_weight': (0.0, 0.1), 'L1_gnn_b_gate': (0.0, 0.1)}
    factors = {}
    for name, (base, spread) in spreads.items():
        noise = np.random.default_rng([zlib.crc32(name.encode()), seed]).standard_normal(out[name].shape)
        drawn = base * np.exp(spread * noise) if base else spread * noise
        out[name] = jnp.asarray(drawn.astype(out[name].dtype))
    for name, factor in factors.items():
        out[name] = (out[name] * factor).astype(out[name].dtype)
    return out
```

```python
from contextlib import ExitStack

import concourse.bass as bass
from concourse import mybir

P = 128
F = 128
HEADS, HD = 4, 32
J = 8
GE = J * P
U = 4
C = 4
PN = 125
NT = C * PN
TW = F + HEADS
K = 4
FW = 500
EPS = 1e-5
SLOPE = 0.2
BIG = 32768.0

ALU = mybir.AluOpType
ACT = mybir.ActivationFunctionType
AX = mybir.AxisListType
F32 = mybir.dt.float32
BF16 = mybir.dt.bfloat16
I32 = mybir.dt.int32


def gnn_kernel(nc, x, src, dst, edge_attr, W, a, W_weight, b_weight, W_gate, b_gate, out):
    N, E = x.shape[0], src.shape[0]
    G = -(-E // (GE * U)) * U
    PAD = N + P
    FULL, REST = E // GE, E % GE
    CH = [(k, min(P, G + 1 - k)) for k in range(0, G + 1, P)]
    T = N // NT
    WINDOWS = -(-N // P)
    GU = G // U
    NZ = -(-N // 2048)
    FIN = N // FW
    assert N % NT == 0 and T % 2 == 1 and PAD < BIG and N % FW == 0
    assert GU >= 2 and FULL >= G - U and len(CH) <= 2 and K * FW <= 2 * GE and J % K == 0

    with ExitStack() as ctx:
        def sb(name, shape, dt=F32):
            return ctx.enter_context(nc.sbuf_tensor(name, shape, dt))

        def sem(name):
            return ctx.enter_context(nc.semaphore(name))

        def sems(name, n):
            return [sem(f"{name}{i}") for i in range(n)]

        def dram(name, shape, dt=F32):
            return nc.dram_tensor(name, shape, dt, kind="Internal").ap()

        table0 = dram("table0", [N, TW])
        score_dst = dram("score_dst", [N + P, HEADS])
        x1 = dram("x1", [N + P, F])
        table_a = dram("table_a", [N, 2 * F])
        table_b = dram("table_b", [N + P, 2 * F])
        acc = [dram(f"acc{k}", [N + P, F]) for k in range(K)]
        pairs = dram("pairs", [G + 1, P, 2 * J], I32)
        digits = dram("digits", [G + 1, 2, 2 * GE], BF16)

        iota_n = sb("iota_n", [P, P])
        iota_p = sb("iota_p", [P, 1])
        dump = sb("dump", [P, 1])
        ident = sb("ident", [P, P])
        ident_b = sb("ident_b", [P, P], BF16)
        later_b = sb("later_b", [P, 4, P], BF16)
        ones = sb("ones", [P, P])
        ones_b = sb("ones_b", [2, P], BF16)
        zeros = sb("zeros", [P, 2048])
        eps = sb("eps", [P, 1])
        w0 = sb("w0", [P, F])
        a_diag = sb("a_diag", [P, 2 * HEADS])
        w0t = sb("w0t", [P, TW + HEADS])
        w_nodes = sb("w_nodes", [P, 4 * F])
        w_edge = sb("w_edge", [P, 2 * F])
        bias_row = sb("bias_row", [1, 2 * F])
        bias = sb("bias", [P, 2 * F])
        ends = sb("ends", [P, 4])
        diag = sb("diag", [P, 4, P])
        base = sb("base", [P, G + 1])
        span = sb("span", [P, G + 1])
        start = sb("start", [P, G + 1])
        span_max = sb("span_max", [P, 1])
        passes_i = sb("passes_i", [P, 3], I32)
        win = sb("win", [P, G + 1])
        win_i = sb("win_i", [P, G + 1], I32)
        node_id = sb("node_id", [P, G + 1])
        xt = sb("xt", [P, 2, C, F])
        stats = sb("stats", [P, 2, C, 6])
        mv = sb("mv", [P, 2, C, 2])
        std = sb("std", [P, 2, C])
        rstd = sb("rstd", [P, 2, C])
        xn = sb("xn", [P, 2, C, F])
        ht = sb("ht", [P, NT])
        t0 = sb("t0", [P, 2, C, TW])
        sd0 = sb("sd0", [P, 2, C, HEADS])
        idx = sb("idx", [P, U, 2 * J], I32)
        rows = sb("rows", [2, U, 2 * GE], BF16)
        sdw = sb("sdw", [P, U, HEADS])
        bw = sb("bw", [P, U, 2 * F])
        ea = sb("ea", [P, U, J * F])
        gat = sb("gat", [P, U, J * 2 * F])
        rel = sb("rel", [P, J])
        above = sb("above", [P, J])
        srcf = sb("srcf", [P, J])
        count = sb("count", [P, J])
        first = sb("first", [P, J])
        shift = sb("shift", [P, J])
        mask = sb("mask", [P, 2, J])
        sidx = sb("sidx", [P, U, J], I32)
        lin = sb("lin", [P, J, HEADS])
        att = sb("att", [P, J, HEADS])
        to_edge = sb("to_edge", [P, 2, GE])
        to_node = sb("to_node", [P, 2, GE])
        msg = sb("msg", [P, 2, GE])
        summed = sb("summed", [P, 2, GE])
        x1w = sb("x1w", [P, 2, F])
        x1o = sb("x1o", [P, 2, F])
        eat = sb("eat", [P, 2, 4 * P])
        pre = sb("pre", [P, J, 2 * F])
        sig = sb("sig", [P, J, F])
        pos = sb("pos", [P, J, F])
        same = to_node

        ps = ctx.enter_context(nc.psum_tensor("ps", [P, 8, 512], F32))
        bc_dst = ps[:, 0:2, :]
        bc_src = ps[:, 2:4, :]
        tp = ps[:, 6, :]
        mm = ps[:, 7, :]

        ab = [gat[:, 2 * s:2 * s + 2, 0:C * 2 * F].rearrange("p h (c f) -> p h c f", c=C) for s in range(2)]

        def prep_int(k):
            return gat[:, k, :].bitcast(I32).rearrange("p (s e) -> p s e", s=2)

        def prep_pairs(k):
            return ea[:, 2 * k:2 * k + 2, :].rearrange("p a b -> p (a b)").bitcast(I32)

        def prep_digits(k):
            return gat[:, 2 + k, :].bitcast(BF16)

        prep_low = pos[:].rearrange("p a b -> p (a b)").bitcast(I32)
        prep_high = sig[:].rearrange("p a b -> p (a b)").bitcast(I32)
        prep_real = msg[:, 0, :]

        consts, weights, w_ps, w_sb = sem("consts"), sem("weights"), sem("w_ps"), sem("w_sb")
        edges_in = sem("edges_in")
        prep_dve, prep_packed, prep_diag, prep_ps = (
            sem("prep_dve"), sem("prep_packed"), sem("prep_diag"), sem("prep_ps"))
        windows_known = sem("windows_known")
        stored = sem("stored")
        x_in, x_stored, t_stored = sems("x_in", 2), sems("x_stored", 2), sems("t_stored", 2)
        node_dve, node_var, node_std, node_xn = sem("node_dve"), sem("node_var"), sem("node_std"), sem("node_xn")
        node_tp, node_ht, node_ps = sem("node_tp"), sem("node_ht"), sem("node_ps")
        node_out, node_out_a = sem("node_out"), sem("node_out_a")
        half_a, half_b = sem("half_a"), sem("half_b")
        nodes_done = sem("nodes_done")
        past_waits = sem("past_waits")
        pass_dve = sem("pass_dve")
        pass_go, pass_done = sems("pass_go", 2), sems("pass_done", 2)
        idx_in = [sems(f"idx_in{l}_", U) for l in range(2)]
        rows_in = [sems(f"rows_in{l}_", U) for l in range(2)]
        gathered = [sems(f"gathered{l}_", U) for l in range(2)]
        sdw_in, bw_in, ea_in = sems("sdw_in", U), sems("bw_in", U), sems("ea_in", U)
        bc0, to_edge0, dve0, expanded = sem("bc0"), sem("to_edge0"), sem("dve0"), sem("expanded")
        msgs0 = sem("msgs0")
        acc_up = sem("acc_up")
        copied0 = sem("copied0")
        x1_in, x1_st = sem("x1_in"), sem("x1_st")
        bc1, to_edge1, dve1, same1, sidx_up = sem("bc1"), sem("to_edge1"), sem("dve1"), sem("same1"), sem("sidx_up")
        ea_tp, ea_t, z_up = sem("ea_tp"), sem("ea_t"), sem("z_up")
        pre_up = sem("pre_up")
        acts = sem("acts")
        m_up = sem("m_up")
        s_up, sum_up = sem("s_up"), sem("sum_up")
        sum_free = sem("sum_free")
        added = sems("added", K)
        fin_in, fin_out = sems("fin_in", U), sems("fin_out", U)
        fin_pool, fin_dve, fin_sum = sem("fin_pool"), sem("fin_dve"), sem("fin_sum")

        N_PADS, N_CONST = 6, 16
        N_WEIGHT = 16 * (1 + 2 * HEADS + 6 + 2)
        N_STORED = 16 * ((K - 1) * NZ + 2 * len(CH))
        FRONT = 7
        STEPS0 = 4

        def node_rows(table, t):
            return table[bass.ds(t * NT, NT), :].rearrange("(p c) f -> p (c f)", c=C)

        def slot_rounds(s, layer):
            return layer * (T // 2 + (1 if s == 0 else 0))

        block = ctx.enter_context(nc.Block())

        @block.sync
        def _(sp):
            sp.wait_ge(consts, N_PADS)
            for k, (g0, n) in enumerate(CH):
                full = max(0, min(n, FULL - g0))
                for s, arr in enumerate((src, dst)):
                    if full:
                        sp.dma_start(prep_int(k)[0:full, s, :], arr[g0 * GE:(g0 + full) * GE].rearrange(
                            "(g e) -> g e", e=GE)).then_inc(edges_in, 16)
                    else:
                        sp.sem_inc(edges_in, 16)
                    if REST and g0 <= FULL < g0 + n:
                        sp.dma_start(prep_int(k)[full:full + 1, s, 0:REST],
                                     arr[FULL * GE:E].rearrange("(g e) -> g e", g=1)).then_inc(edges_in, 16)
                    else:
                        sp.sem_inc(edges_in, 16)
            sp.dma_start(w0[:], W).then_inc(weights, 16)
            for h in range(HEADS):
                for i in range(2):
                    sp.dma_start(a_diag[h * HD:(h + 1) * HD, i * HEADS + h:i * HEADS + h + 1],
                                 a[h:h + 1, i * HD:(i + 1) * HD].rearrange("o d -> d o")).then_inc(weights, 16)
            for i, w in enumerate((W_weight, W_gate)):
                sp.dma_start(w_nodes[:, i * F:(i + 1) * F], w[0:F, :]).then_inc(weights, 16)
                sp.dma_start(w_nodes[:, (2 + i) * F:(3 + i) * F], w[F:2 * F, :]).then_inc(weights, 16)
                sp.dma_start(w_edge[:, i * F:(i + 1) * F], w[2 * F:3 * F, :]).then_inc(weights, 16)
            for i, b in enumerate((b_weight, b_gate)):
                sp.dma_start(bias_row[:, i * F:(i + 1) * F], b.rearrange("(o f) -> o f", o=1)).then_inc(weights, 16)
            for k, (g0, n) in enumerate(CH):
                sp.wait_ge(prep_packed, k + 1)
                sp.dma_start(pairs[g0:g0 + n].rearrange("g p s -> g (p s)"), prep_pairs(k)[0:n, :]).then_inc(stored, 16)
                sp.dma_start(digits[g0:g0 + n].rearrange("g d e -> g (d e)"),
                             prep_digits(k)[0:n, :]).then_inc(stored, 16)

            def load_nodes(layer, t, i, s):
                sp.wait_ge(x_stored[s], 16 * (i + slot_rounds(s, layer) + 1))
                sp.dma_start(xt[0:PN, s].rearrange("p c f -> p (c f)"),
                             node_rows(x1 if layer else x, t)).then_inc(x_in[s], 16)

            def load_front(layer, g, s, pads=False):
                sp.dma_start(rows[:, s, :], digits[bass.ds(g, 1)].rearrange(
                    "g d e -> (g d) e")).then_inc(rows_in[layer][s], 16)
                if layer == 1 or not pads:
                    sp.dma_start(idx[:, s, :], pairs[bass.ds(g, 1)].rearrange(
                        "g p s -> (g p) s")).then_inc(idx_in[layer][s], 16)

            def load_window(layer, g, s):
                start = sp.value_load(win_i[0:1, bass.ds(g, 1)], min_val=0, max_val=N)
                if layer == 0:
                    sp.dma_start(sdw[:, s, :], score_dst[bass.ds(start, P), :]).then_inc(sdw_in[s], 16)
                else:
                    sp.dma_start(bw[:, s, :], table_b[bass.ds(start, P), :]).then_inc(bw_in[s], 16)

            def load_edges(g, s, n):
                whole, part = n // J, n % J
                if n == GE:
                    whole, part = P // 2, J
                last = whole + (P // 2 if n == GE else 1)
                rows_of = edge_attr[bass.ds(g * GE, n), :] if n else None
                if whole:
                    sp.dma_start(ea[0:whole, s, :], rows_of[0:whole * J, :].rearrange(
                        "(p j) f -> p (j f)", j=J)).then_inc(ea_in[s], 16)
                else:
                    sp.sem_inc(ea_in[s], 16)
                if part:
                    sp.dma_start(ea[whole:last, s, 0:part * F], rows_of[whole * J:n, :].rearrange(
                        "(p j) f -> p (j f)", j=part)).then_inc(ea_in[s], 16)
                else:
                    sp.sem_inc(ea_in[s], 16)

            def edge_loads(layer, passes):
                free = msgs0 if layer == 0 else m_up
                per = 1 if layer == 0 else 2
                with sp.Fori(0, passes) as w:
                    sp.wait_ge(pass_go[layer], w + 1)
                    sp.sem_inc(past_waits, 1)
                    with sp.Fori(0, GU - layer) as i:
                        for s in range(U):
                            sp.wait_ge(free, per * (U * (w * GU + i) + s + 1))
                            load_front(layer, U * i + s, s)
                            load_window(layer, U * i + s, s)
                            if layer == 1:
                                load_edges(U * i + s, s, GE)
                    if layer == 1:
                        for s in range(U):
                            g = G - U + s
                            sp.wait_ge(free, per * (w * G + g + 1))
                            load_front(layer, g, s)
                            load_window(layer, g, s)
                            load_edges(g, s, GE if g < FULL else REST if g == FULL else 0)
                    sp.wait_ge(free, per * (w * G + G + 1))
                    load_front(layer, G, 0, pads=True)

            for layer in range(2):
                if layer == 1:
                    sp.wait_ge(pass_done[0], 2 * passes + 1)
                    sp.sem_inc(past_waits, 1)
                with sp.Fori(0, T // 2) as i:
                    for s in range(2):
                        load_nodes(layer, 2 * i + s, i, s)
                load_nodes(layer, T - 1, T // 2, 0)
                if layer == 0:
                    sp.wait_ge(windows_known, 1)
                    passes = sp.value_load(passes_i[0:1, 2:3], min_val=1, max_val=WINDOWS)
                sp.wait_ge(nodes_done, layer + 1)
                edge_loads(layer, passes)

            sp.wait_ge(pass_done[1], passes + 1)
            for n in range(FIN):
                if n >= U:
                    sp.wait_ge(fin_out[n % U], 16 * (n // U))
                for k in range(K):
                    flat = acc[k][0:N, :].rearrange("n f -> (n f)").rearrange("(p e) -> p e", p=P)
                    sp.dma_start(gat[:, n % U, k * FW:(k + 1) * FW],
                                 flat[:, n * FW:(n + 1) * FW]).then_inc(fin_in[n % U], 16)

        @block.gpsimd
        def _(pool):
            pool.sem_inc(pass_done[1], 1)
            step = [0]

            def const(ins):
                step[0] += 1
                ins.then_inc(consts, 1)
                pool.wait_ge(consts, step[0])

            const(nc.gpsimd.memset(zeros[:], 0.0))
            for k in range(K):
                pool.dma_start(acc[k][N:N + P, :], zeros[:, 0:F]).then_inc(added[k], 16)
            for s in range(2):
                half, quarter = N + P // 2 * s, N + P // 4 * s
                pool.dma_start(x1[quarter:quarter + P // 4, :], zeros[0:P // 4, 0:F]).then_inc(x_stored[s], 16)
                pool.dma_start(score_dst[half:half + P // 2, :], zeros[0:P // 2, 0:HEADS]).then_inc(t_stored[s], 16)
                pool.dma_start(table_b[half:half + P // 2, :], zeros[0:P // 2, 0:2 * F]).then_inc(t_stored[s], 16)
            const(nc.gpsimd.memset(a_diag[:], 0.0))
            for k in range(2):
                const(nc.gpsimd.memset(gat[:, k, 0:GE].bitcast(I32), 0))
                const(nc.gpsimd.memset(gat[:, k, GE:2 * GE].bitcast(I32), PAD))
            const(nc.gpsimd.memset(ones[:], 1.0))
            const(nc.gpsimd.memset(ones_b[:], 1.0))
            const(nc.gpsimd.memset(eps[:], EPS))
            const(nc.gpsimd.iota(iota_n[:], [[1, P]], base=0, channel_multiplier=0,
                                 allow_small_or_imprecise_dtypes=True))
            const(nc.gpsimd.iota(iota_p[:], [[0, 1]], base=0, channel_multiplier=1,
                                 allow_small_or_imprecise_dtypes=True))
            const(nc.gpsimd.affine_select(out=ident[:], in_=ones[:], pattern=[[-1, P]], compare_op=ALU.is_equal,
                                          fill=0.0, base=0, channel_multiplier=1))
            const(nc.gpsimd.memset(later_b[:], BIG))
            const(nc.gpsimd.affine_select(out=later_b[:], in_=later_b[:], pattern=[[0, 4], [1, P]],
                                          compare_op=ALU.is_gt, fill=0.0, base=0, channel_multiplier=-1))
            const(nc.gpsimd.iota(dump[:], [[0, 1]], base=N, channel_multiplier=1,
                                 allow_small_or_imprecise_dtypes=True))
            const(nc.gpsimd.tensor_copy(ident_b[:], ident[:]))
            assert step[0] == N_CONST

            def store_nodes(layer, t, i, s):
                r = i + slot_rounds(s, layer)
                n = t + layer * T
                pool.wait_ge(node_xn, n + 1)
                pool.sem_inc(past_waits, 1)
                pool.dma_start(node_rows(acc[0] if layer else x1, t),
                               xt[0:PN, s].rearrange("p c f -> p (c f)")).then_inc(x_stored[s], 16)
                pool.wait_ge(node_out, n + 2)
                pool.sem_inc(past_waits, 1)
                if layer == 0:
                    pool.dma_start(node_rows(table0, t),
                                   t0[0:PN, s].rearrange("p c f -> p (c f)")).then_inc(t_stored[s], 16)
                    pool.dma_start(node_rows(score_dst, t),
                                   sd0[0:PN, s].rearrange("p c f -> p (c f)")).then_inc(t_stored[s], 16)
                else:
                    pool.dma_start(node_rows(table_b, t),
                                   ab[s][0:PN, 1].rearrange("p c f -> p (c f)")).then_inc(t_stored[s], 16)
                    pool.wait_ge(node_out_a, t + 2)
                    pool.sem_inc(past_waits, 1)
                    pool.dma_start(node_rows(table_a, t),
                                   ab[s][0:PN, 0].rearrange("p c f -> p (c f)")).then_inc(t_stored[s], 16)

            def gather(layer, s, table, width):
                pool.sem_inc(past_waits, 1)
                for j in range(J):
                    nc.gpsimd.indirect_dma_start(
                        out=gat[:, s, j * width:(j + 1) * width], out_offset=None, in_=table,
                        in_offset=bass.IndirectOffsetOnAxis(ap=idx[:, s, j:j + 1], axis=0),
                    ).then_inc(gathered[layer][s], 16)

            for layer in range(2):
                with pool.Fori(0, T // 2) as i:
                    for s in range(2):
                        store_nodes(layer, 2 * i + s, i, s)
                store_nodes(layer, T - 1, T // 2, 0)
                for s in range(2):
                    pool.wait_ge(x_stored[s], 16 * (slot_rounds(s, layer + 1) + 1))
                    pool.wait_ge(t_stored[s], 32 * (slot_rounds(s, layer + 1) + 1))
                if layer == 0:
                    pool.wait_ge(stored, N_STORED)
                    pool.wait_ge(windows_known, 1)
                    passes = pool.value_load(passes_i[0:1, 2:3], min_val=1, max_val=WINDOWS)
                pool.sem_inc(nodes_done, 1)

                if layer == 0:
                    with pool.Fori(0, passes) as w:
                        with pool.Fori(0, GU) as i:
                            turn = pool.snap(w * GU + i)
                            for s in range(U):
                                pool.wait_ge(msgs0, U * turn + s + 1)
                                pool.wait_ge(idx_in[0][s], 16 * (turn + 1))
                                gather(0, s, table0, TW)
                    continue

                with pool.Fori(0, passes) as w:
                    pool.wait_ge(pass_go[1], w + 1)
                    pool.wait_ge(idx_in[1][0], 16 * (w * GU + w + 1))
                    gather(1, 0, table_a, 2 * F)
                    with pool.Fori(0, GU) as i:
                        turn = pool.snap(w * GU + i)
                        for s in range(U):
                            q = U * turn + s
                            nxt = (s + 1) % U
                            pool.wait_ge(m_up, 2 * (q + 2))
                            pool.wait_ge(idx_in[1][nxt], 16 * ((turn + w + 2) if nxt == 0 else (turn + 1)))
                            gather(1, nxt, table_a, 2 * F)
                            pool.wait_ge(sidx_up, q + w + 1)
                            for j in range(J):
                                if j % (J // 2) == 0:
                                    pool.wait_ge(sum_up, 2 * q + j // (J // 2) + 2)
                                pool.wait_ge(added[j % K], 16 * ((J // K) * q + j // K + 1))
                                if j == K:
                                    pool.sem_inc(sum_free, 1)
                                else:
                                    pool.sem_inc(past_waits, 1)
                                nc.gpsimd.indirect_dma_start(
                                    out=acc[j % K], out_offset=bass.IndirectOffsetOnAxis(
                                        ap=sidx[:, s, j:j + 1], axis=0),
                                    in_=summed[:, s % 2, j * F:(j + 1) * F], in_offset=None,
                                    bounds_check=N + P - 1, oob_is_err=True,
                                    compute_op=ALU.add).then_inc(added[j % K], 16)
                    for k in range(K):
                        pool.wait_ge(added[k], 16 * ((J // K) * (w * G + G) + 1))
                    pool.wait_ge(gathered[1][0], 16 * J * (w * GU + GU + w + 1))
                    pool.sem_inc(pass_done[1], 1)

            for n in range(FIN):
                s = n % U
                pool.wait_ge(fin_in[s], 16 * K * (n // U + 1))
                nc.gpsimd.tensor_tensor(gat[:, s, 2 * FW:3 * FW], gat[:, s, 2 * FW:3 * FW],
                                        gat[:, s, 3 * FW:4 * FW], ALU.add).then_inc(fin_pool, 1)

        @block.tensor
        def _(pe):
            pe.sem_inc(acc_up, 2)
            pe.wait_ge(consts, N_CONST)
            pe.wait_ge(weights, N_WEIGHT)
            pe.transpose(ps[:, 0, 0:F], w0[:], ident[:])
            pe.matmul(ps[:, 1, 0:2 * HEADS], w0[:], a_diag[:], start=True, stop=True)
            pe.matmul(ps[:, 2, 0:2 * F], ones[0:1, :], bias_row[:], start=True, stop=True).then_inc(w_ps, 1)
            pe.wait_ge(prep_diag, 1)
            for c in range(4):
                mmi = pe.matmul(ps[:, 4 + c // 2, (c % 2) * P:(c % 2) * P + P], ones[:], diag[:, c, :],
                                start=True, stop=True)
            mmi.then_inc(prep_ps, 1)
            pe.wait_ge(w_sb, 3)
            pe.wait_ge(windows_known, 1)
            passes = pe.value_load(passes_i[0:1, 2:3], min_val=1, max_val=WINDOWS)

            def node_products(layer, t, s):
                n = t + layer * T
                pe.wait_ge(node_xn, n + 1)
                for c in range(C):
                    mmi = pe.transpose(tp[:, c * PN:(c + 1) * PN], xn[0:PN, s, c, :], ident[0:PN, 0:PN])
                mmi.then_inc(node_tp, 1)
                pe.wait_ge(node_ht, n + 1)
                pe.wait_ge(node_out, n + 1)
                if layer == 1:
                    pe.wait_ge(node_out_a, t + 1)
                wt, width = (w0t, TW + HEADS) if layer == 0 else (w_nodes, 4 * F)
                for c in range(C):
                    mmi = pe.matmul(ps[0:PN, c, 0:width], ht[:, c * PN:(c + 1) * PN], wt[:, 0:width],
                                    start=True, stop=True)
                mmi.then_inc(node_ps, 1)

            def nodes(layer):
                with pe.Fori(0, T // 2) as i:
                    for s in range(2):
                        node_products(layer, 2 * i + s, s)
                node_products(layer, T - 1, 0)

            nodes(0)
            pe.wait_ge(node_out, T + 1)

            def spread_dst0(s, f, q):
                pe.wait_ge(rows_in[0][s], f)
                pe.wait_ge(to_edge0, q + 1)
                for b in range(2):
                    mmi = pe.matmul(bc_dst[:, b, :], ones_b[:], rows[:, s, GE + 512 * b:GE + 512 * (b + 1)],
                                    start=True, stop=True)
                mmi.then_inc(bc0, 1)

            with pe.Fori(0, passes) as w:
                spread_dst0(0, 16 * (w * GU + w + 1), w * G)
                with pe.Fori(0, GU) as i:
                    turn = pe.snap(w * GU + i)
                    for s in range(U):
                        q = U * turn + s
                        pe.wait_ge(to_edge0, q + 2)
                        pe.wait_ge(sdw_in[s], 16 * (turn + 1))
                        for j in range(J):
                            mmi = pe.matmul(ps[:, 6 + s % 2, j * HEADS:(j + 1) * HEADS],
                                            to_edge[:, 0, j * P:(j + 1) * P], sdw[:, s, :], start=True, stop=True)
                        mmi.then_inc(expanded, 1)
                        nxt = (s + 1) % U
                        spread_dst0(nxt, 16 * ((turn + w + 2) if nxt == 0 else (turn + 1)), q + 1)
                        pe.wait_ge(x1_in, 16 * (q + 1))
                        pe.wait_ge(copied0, q + 1)
                        pe.wait_ge(msgs0, q + 1 + U)
                        out_ps = ps[:, 4 + s % 2, 0:F]
                        pe.matmul(out_ps, ident[:], x1w[:, s % 2, :], start=True, stop=False)
                        for j in range(J):
                            mmi = pe.matmul(out_ps, to_node[:, s % 2, j * P:(j + 1) * P],
                                            msg[:, s % 2, j * F:(j + 1) * F], start=False, stop=(j == J - 1))
                        mmi.then_inc(acc_up, 1)
                pe.wait_ge(bc0, w * G + G + w + 1)
                pe.sem_inc(pass_done[0], 1)

            nodes(1)
            pe.wait_ge(node_out, 2 * T + 1)
            pe.wait_ge(node_out_a, T + 1)

            def spread1(s, f, done):
                pe.wait_ge(rows_in[1][s], f)
                pe.wait_ge(same1, done + 1)
                for b in range(2):
                    mmi = pe.matmul(bc_dst[:, b, :], ones_b[:], rows[:, s, GE + 512 * b:GE + 512 * (b + 1)],
                                    start=True, stop=True)
                mmi.then_inc(bc1, 1)
                for b in range(2):
                    pe.matmul(bc_src[:, b, :], ones_b[:], rows[:, s, 512 * b:512 * (b + 1)], start=True, stop=False)
                    mmi = pe.matmul(bc_src[:, b, :], ident_b[:], later_b[:].rearrange("p t n -> p (t n)"),
                                    start=False, stop=True)
                mmi.then_inc(bc1, 1)

            with pe.Fori(0, passes) as w:
                spread1(0, 16 * (w * GU + w + 1), w * G + w)
                with pe.Fori(0, GU) as i:
                    turn = pe.snap(w * GU + i)
                    for s in range(U):
                        q = U * turn + s
                        pe.wait_ge(ea_in[s], 32 * (turn + 1))
                        for h in range(2):
                            pe.wait_ge(ea_t, 2 * q + h + 1)
                            for j in range(4 * h, 4 * h + 4):
                                mmi = pe.transpose(tp[:, (j % 4) * P:(j % 4 + 1) * P],
                                                   ea[:, s, j * F:(j + 1) * F], ident[:])
                            mmi.then_inc(ea_tp, 1)
                        pe.wait_ge(to_edge1, q + w + 1)
                        pe.wait_ge(bw_in[s], 16 * (turn + 1))
                        for k in range(4):
                            if k % 2 == 0:
                                pe.wait_ge(ea_t, 2 * q + k // 2 + 2)
                            pe.wait_ge(pre_up, 4 * q + k + 1)
                            for j in range(2 * k, 2 * k + 2):
                                z = ps[:, 4 + k % 2, (j % 2) * 2 * F:(j % 2 + 1) * 2 * F]
                                pe.matmul(z, eat[:, j // 4, (j % 4) * P:(j % 4 + 1) * P], w_edge[:],
                                          start=True, stop=False)
                                mmi = pe.matmul(z, to_edge[:, s % 2, j * P:(j + 1) * P], bw[:, s, :],
                                                start=False, stop=True)
                            mmi.then_inc(z_up, 1)
                        nxt = (s + 1) % U
                        spread1(nxt, 16 * ((turn + w + 2) if nxt == 0 else (turn + 1)), q + w + 1)
                        for h in range(2):
                            pe.wait_ge(m_up, 2 * U + 2 * q + h + 1)
                            pe.wait_ge(sum_up, 2 * q + h + 1)
                            for j in range(4 * h, 4 * h + 4):
                                mmi = pe.matmul(mm[:, (j % 4) * F:(j % 4 + 1) * F],
                                                same[:, s % 2, j * P:(j + 1) * P],
                                                msg[:, 0, j * F:(j + 1) * F], start=True, stop=True)
                            mmi.then_inc(s_up, 1)

        @block.scalar
        def _(act):
            act.sem_inc(copied0, 2)
            act.sem_inc(pass_done[0], 1)
            for one in (ea_t, sum_up, node_out_a):
                act.sem_inc(one, 1)
            act.wait_ge(consts, 1)
            act.dma_start(x1[N + P // 2:N + P, :], zeros[0:P // 2, 0:F]).then_inc(x1_st, 16)
            for k in range(1, K):
                flat = acc[k][0:N, :].rearrange("n f -> (n f)").rearrange("(p e) -> p e", p=P)
                for c in range(0, N, 2048):
                    n = min(2048, N - c)
                    act.dma_start(flat[:, c:c + n], zeros[:, 0:n]).then_inc(stored, 16)
            act.wait_ge(windows_known, 1)
            passes = act.value_load(passes_i[0:1, 2:3], min_val=1, max_val=WINDOWS)

            def root(n, s):
                act.wait_ge(node_var, n + 1)
                nc.scalar.activation(std[0:PN, s, :], mv[0:PN, s, :, 1], ACT.Sqrt,
                                     bias=eps[0:PN, :]).then_inc(node_std, 1)

            def relu_out(layer, t, i, s):
                n = t + layer * T
                act.wait_ge(node_tp, n + 1)
                nc.scalar.activation(ht[:], tp[:, 0:NT], ACT.Relu).then_inc(node_ht, 1)

            def out_a(t, i, s):
                act.wait_ge(t_stored[s], 32 * (i + slot_rounds(s, 1) + 1))
                act.wait_ge(node_ps, t + T + 1)
                nc.scalar.activation(ab[s][0:PN, 0, 0:2], ps[0:PN, 0:2, 0:2 * F], ACT.Copy).then_inc(half_a, 1)
                act.wait_ge(half_b, t + 1)
                nc.scalar.activation(ab[s][0:PN, 0, 2:C], ps[0:PN, 2:C, 0:2 * F], ACT.Copy).then_inc(node_out_a, 1)

            def nodes(layer):
                root(layer * T, 0)
                with act.Fori(0, T // 2) as i:
                    for s in range(2):
                        relu_out(layer, 2 * i + s, i, s)
                        root(2 * i + s + 1 + layer * T, 1 - s)
                        if layer == 1:
                            out_a(2 * i + s, i, s)
                relu_out(layer, T - 1, T // 2, 0)
                if layer == 1:
                    out_a(T - 1, T // 2, 0)

            nodes(0)
            act.wait_ge(nodes_done, 1)
            with act.Fori(0, passes) as w:
                act.wait_ge(pass_go[0], w + 1)
                with act.Fori(0, GU) as i:
                    turn = act.snap(w * GU + i)
                    for s in range(U):
                        q = U * turn + s
                        start = act.value_load(win_i[0:1, bass.ds(U * i + s, 1)], min_val=0, max_val=N)
                        act.wait_ge(x1_st, 16 * (q + 1))
                        act.dma_start(x1w[:, s % 2, :], x1[bass.ds(start, P), :]).then_inc(x1_in, 16)
                        act.wait_ge(acc_up, q + 3)
                        nc.scalar.activation(x1o[:, s % 2, :], ps[:, 4 + s % 2, 0:F], ACT.Copy).then_inc(copied0, 1)
                        act.wait_ge(copied0, q + 3)
                        act.dma_start(x1[bass.ds(start, P), :], x1o[:, s % 2, :]).then_inc(x1_st, 16)
                act.wait_ge(x1_st, 16 * (w * G + G + 1))
                act.sem_inc(pass_done[0], 1)

            nodes(1)
            with act.Fori(0, passes) as w:
                with act.Fori(0, GU) as i:
                    turn = act.snap(w * GU + i)
                    for s in range(U):
                        q = U * turn + s
                        for h in range(2):
                            act.wait_ge(ea_tp, 2 * q + h + 1)
                            nc.scalar.activation(eat[:, h, :], tp, ACT.Copy).then_inc(ea_t, 1)
                        for h in range(2):
                            act.wait_ge(pre_up, 4 * q + 2 * (h + 1) + 2)
                            for j in range(4 * h, 4 * h + 4):
                                nc.scalar.activation(pos[:, j, :], pre[:, j, 0:F], ACT.Relu,
                                                     scale=mask[:, s % 2, j:j + 1])
                            nc.scalar.activation(sig[:, 4 * h:4 * h + 4, :], pre[:, 4 * h:4 * h + 4, F:2 * F],
                                                 ACT.Sigmoid).then_inc(acts, 1)
                        act.wait_ge(sum_free, q + 2)
                        for h in range(2):
                            act.wait_ge(s_up, 2 * q + h + 1)
                            nc.scalar.activation(summed[:, s % 2, 512 * h:512 * (h + 1)], mm,
                                                 ACT.Copy).then_inc(sum_up, 1)

            for n in range(FIN):
                flat = out.rearrange("n f -> (n f)").rearrange("(p e) -> p e", p=P)
                act.wait_ge(fin_sum, n + 1)
                act.dma_start(flat[:, n * FW:(n + 1) * FW], gat[:, n % U, 0:FW]).then_inc(fin_out[n % U], 16)
            for s in range(U):
                act.wait_ge(fin_out[s], 16 * len(range(s, FIN, U)))

        @block.vector
        def _(dve):
            dve.sem_inc(msgs0, U)
            dve.sem_inc(pre_up, 2)
            dve.sem_inc(m_up, 2 * U)
            dve.sem_inc(sum_free, 2)
            for one in (node_out, to_edge0, same1):
                dve.sem_inc(one, 1)
            step = [0]

            def link(ins):
                step[0] += 1
                ins.then_inc(prep_dve, 1)
                dve.wait_ge(prep_dve, step[0])

            dve.wait_ge(edges_in, 64 * len(CH))
            link(nc.vector.memset(ends[:], 0.0))
            for k, (g0, n) in enumerate(CH):
                for s in range(2):
                    e = prep_int(k)[:, s, :]
                    link(nc.vector.tensor_copy(
                        prep_pairs(k).rearrange("g (p s j) -> g p s j", s=2, j=J)[:, :, s, :],
                        e.rearrange("g (p j) -> g p j", j=J)))
                    link(nc.vector.tensor_scalar(prep_low, e, P - 1, None, ALU.bitwise_and))
                    link(nc.vector.tensor_tensor(prep_high, e, prep_low, ALU.subtract))
                    for d, digit in enumerate((prep_high, prep_low)):
                        link(nc.vector.tensor_copy(
                            prep_digits(k).rearrange("g (d s j p) -> g d s p j", d=2, s=2, j=J)[:, d, s],
                            digit.rearrange("g (p j) -> g p j", j=J)))
                dve.sem_inc(prep_packed, 1)
                e = prep_int(k)[:, 1, :]
                link(nc.vector.tensor_reduce(ends[:, k:k + 1], e, AX.X, ALU.min))
                link(nc.vector.scalar_tensor_tensor(prep_real, e, float(N), e, ALU.is_lt, ALU.mult))
                link(nc.vector.tensor_reduce(ends[:, 2 + k:3 + k], prep_real, AX.X, ALU.max))
            link(nc.vector.tensor_tensor(ends[:, 2:4], ends[:, 2:4], ends[:, 0:2], ALU.subtract))
            dve.wait_ge(consts, N_CONST)
            for c in range(4):
                link(nc.vector.tensor_scalar(diag[:, c, :], ident[:], ends[:, c:c + 1], None, ALU.mult))
            dve.sem_inc(prep_diag, 1)
            dve.wait_ge(w_ps, 1)
            nc.vector.tensor_copy(w0t[:, 0:F], ps[:, 0, 0:F]).then_inc(w_sb, 1)
            nc.vector.tensor_copy(w0t[:, F:TW + HEADS], ps[:, 1, 0:2 * HEADS]).then_inc(w_sb, 1)
            nc.vector.tensor_copy(bias[:], ps[:, 2, 0:2 * F]).then_inc(w_sb, 1)
            dve.wait_ge(prep_ps, 1)
            for k, (g0, n) in enumerate(CH):
                link(nc.vector.tensor_copy(base[:, g0:g0 + n], ps[:, 4, k * P:k * P + n]))
                link(nc.vector.tensor_copy(span[:, g0:g0 + n], ps[:, 5, k * P:k * P + n]))
            link(nc.vector.tensor_reduce(span_max[:], span[:], AX.X, ALU.max))
            link(nc.vector.tensor_copy(passes_i[:, 0:1], span_max[:]))
            link(nc.vector.tensor_scalar(passes_i[:, 1:2], passes_i[:, 0:1], 7, None, ALU.arith_shift_right))
            link(nc.vector.tensor_scalar(passes_i[:, 2:3], passes_i[:, 1:2], 1.0, None, ALU.add))
            dve.sem_inc(windows_known, 1)
            passes = dve.value_load(passes_i[0:1, 2:3], min_val=1, max_val=WINDOWS)

            def normalise(layer, t, i, s):
                n = t + layer * T
                dve.wait_ge(x_in[s], 16 * (i + slot_rounds(s, layer) + 1))
                for c in range(C):
                    ins = nc.vector.bn_stats(stats[0:PN, s, c, :], xt[0:PN, s, c, :])
                ins.then_inc(node_dve, 1)
                dve.wait_ge(node_dve, 2 * n + 1)
                dve.sem_inc(past_waits, 1)
                for c in range(C):
                    ins = nc.vector.bn_aggr(mv[0:PN, s, c, :], stats[0:PN, s, c, :])
                ins.then_inc(node_var, 1)
                dve.wait_ge(node_std, n + 1)
                nc.vector.reciprocal(rstd[0:PN, s, :], std[0:PN, s, :]).then_inc(node_dve, 1)
                dve.wait_ge(node_dve, 2 * n + 2)
                for c in range(C):
                    ins = nc.vector.tensor_scalar(xn[0:PN, s, c, :], xt[0:PN, s, c, :], mv[0:PN, s, c, 0:1],
                                                  rstd[0:PN, s, c:c + 1], ALU.subtract, ALU.mult)
                ins.then_inc(node_xn, 1)

            def node_outs(layer, t, i, s):
                dve.wait_ge(t_stored[s], 32 * (i + slot_rounds(s, layer) + 1))
                dve.wait_ge(node_ps, t + layer * T + 1)
                if layer == 0:
                    nc.vector.tensor_copy(t0[0:PN, s], ps[0:PN, 0:C, 0:TW])
                    nc.vector.tensor_copy(sd0[0:PN, s], ps[0:PN, 0:C, TW:TW + HEADS]).then_inc(node_out, 1)
                else:
                    bias_rows = bias[0:PN, :].unsqueeze(1).to_broadcast([PN, 2, 2 * F])
                    nc.vector.tensor_tensor(ab[s][0:PN, 1, 2:C], ps[0:PN, 2:C, 2 * F:4 * F], bias_rows,
                                            ALU.add).then_inc(half_b, 1)
                    dve.wait_ge(half_a, t + 1)
                    nc.vector.tensor_tensor(ab[s][0:PN, 1, 0:2], ps[0:PN, 0:2, 2 * F:4 * F], bias_rows,
                                            ALU.add).then_inc(node_out, 1)

            def nodes(layer):
                normalise(layer, 0, 0, 0)
                with dve.Fori(0, T // 2) as i:
                    normalise(layer, 2 * i + 1, i, 1)
                    node_outs(layer, 2 * i, i, 0)
                    normalise(layer, 2 * i + 2, i + 1, 0)
                    node_outs(layer, 2 * i + 1, i, 1)
                node_outs(layer, T - 1, T // 2, 0)

            def windows(layer, w, steps):
                if layer == 0:
                    dve.wait_ge(pass_done[0], 2 * w + 1)
                else:
                    dve.wait_ge(pass_done[1], w + 1)
                nc.vector.tensor_scalar(win[:], start[:], float(N), None, ALU.min).then_inc(pass_dve, 1)
                dve.wait_ge(pass_dve, steps + 1)
                nc.vector.tensor_copy(win_i[:], win[:]).then_inc(pass_dve, 1)
                nc.vector.tensor_scalar(node_id[:], win[:], iota_p[:, 0:1], None, ALU.add).then_inc(pass_dve, 1)
                nc.vector.tensor_scalar(start[:], start[:], float(P), None, ALU.add).then_inc(pass_dve, 1)
                dve.wait_ge(pass_dve, steps + 4)
                dve.sem_inc(pass_go[layer], 1)

            def by_tile(ap):
                return ap.unsqueeze(2).to_broadcast([P, J, P])

            nodes(0)
            link(nc.vector.tensor_copy(start[:], base[:]))
            with dve.Fori(0, passes) as w:
                windows(0, w, 4 * w)
                with dve.Fori(0, GU) as i:
                    turn = dve.snap(w * GU + i)
                    for s in range(U):
                        q = U * turn + s
                        g = U * i + s
                        dve.wait_ge(bc0, q + w + 1)
                        nc.vector.tensor_scalar(to_edge[:, 0, :], bc_dst.rearrange("p b n -> p (b n)"),
                                                node_id[:, bass.ds(g, 1)], None, ALU.is_equal).then_inc(to_edge0, 1)
                        dve.wait_ge(idx_in[0][s], 16 * (turn + 1))
                        nc.vector.tensor_scalar(rel[:], idx[:, s, J:2 * J], win[:, bass.ds(g, 1)], None,
                                                ALU.subtract).then_inc(dve0, 1)
                        dve.wait_ge(dve0, STEPS0 * q + 1)
                        dve.wait_ge(acc_up, q + 1)
                        nc.vector.tensor_tensor(to_node[:, s % 2, :].rearrange("p (j n) -> p j n", j=J),
                                                iota_n[:].unsqueeze(1).to_broadcast([P, J, P]), by_tile(rel[:]),
                                                ALU.is_equal).then_inc(dve0, 1)
                        row = gat[:, s, 0:J * TW].rearrange("p (j f) -> p j f", j=J)
                        dve.wait_ge(expanded, q + 1)
                        dve.wait_ge(gathered[0][s], 16 * J * (turn + 1))
                        nc.vector.tensor_tensor(lin[:], ps[:, 6 + s % 2, 0:J * HEADS].rearrange(
                            "p (j h) -> p j h", j=J), row[:, :, F:TW], ALU.add).then_inc(dve0, 1)
                        dve.wait_ge(dve0, STEPS0 * q + 3)
                        nc.vector.scalar_tensor_tensor(att[:], lin[:], SLOPE, lin[:], ALU.mult,
                                                       ALU.max).then_inc(dve0, 1)
                        dve.wait_ge(dve0, STEPS0 * q + 4)
                        nc.vector.tensor_tensor(
                            msg[:, s % 2, :].rearrange("p (j h d) -> p j h d", j=J, h=HEADS),
                            row[:, :, 0:F].rearrange("p j (h d) -> p j h d", h=HEADS),
                            att[:].unsqueeze(3).to_broadcast([P, J, HEADS, HD]), ALU.mult).then_inc(msgs0, 1)

            nodes(1)
            link(nc.vector.tensor_copy(start[:], base[:]))

            def front(w, g, s, f, r):
                at = FRONT * f
                dve.wait_ge(bc1, 2 * f + 1)
                nc.vector.tensor_scalar(to_edge[:, s % 2, :], bc_dst.rearrange("p b n -> p (b n)"),
                                        node_id[:, bass.ds(g, 1)], None, ALU.is_equal).then_inc(to_edge1, 1)
                dve.wait_ge(idx_in[1][s], 16 * (r + 1))
                nc.vector.tensor_copy(srcf[:], idx[:, s, 0:J]).then_inc(dve1, 1)
                nc.vector.tensor_scalar(rel[:], idx[:, s, J:2 * J], win[:, bass.ds(g, 1)], None,
                                        ALU.subtract).then_inc(dve1, 1)
                dve.wait_ge(dve1, at + 1)
                dve.wait_ge(bc1, 2 * f + 2)
                nc.vector.tensor_tensor(same[:, s % 2, :].rearrange("p (j n) -> p j n", j=J),
                                        bc_src.rearrange("p b (t n) -> p (b t) n", t=4), by_tile(srcf[:]),
                                        ALU.is_equal).then_inc(same1, 1)
                dve.wait_ge(dve1, at + 2)
                nc.vector.tensor_scalar(above[:], rel[:], 0.0, None, ALU.is_ge).then_inc(dve1, 1)
                dve.wait_ge(dve1, at + 3)
                nc.vector.scalar_tensor_tensor(mask[:, s % 2, :], rel[:], float(P), above[:], ALU.is_lt,
                                               ALU.mult).then_inc(dve1, 1)
                dve.wait_ge(same1, f + 2)
                nc.vector.tensor_reduce(count[:], same[:, s % 2, :].rearrange("p (j n) -> p j n", j=J), AX.X,
                                        ALU.add).then_inc(dve1, 1)
                dve.wait_ge(dve1, at + 5)
                nc.vector.tensor_scalar(first[:], count[:], 1.0, None, ALU.is_equal).then_inc(dve1, 1)
                dve.wait_ge(dve1, at + 6)
                nc.vector.scalar_tensor_tensor(shift[:], srcf[:], dump[:, 0:1], first[:], ALU.subtract,
                                               ALU.mult).then_inc(dve1, 1)
                dve.wait_ge(dve1, at + 7)
                nc.vector.tensor_scalar(sidx[:, s, :], shift[:], dump[:, 0:1], None, ALU.add).then_inc(sidx_up, 1)

            with dve.Fori(0, passes) as w:
                windows(1, w, 4 * (passes + w))
                front(w, 0, 0, w * G + w, w * GU + w)
                with dve.Fori(0, GU) as i:
                    turn = dve.snap(w * GU + i)
                    for s in range(U):
                        q = U * turn + s
                        dve.wait_ge(gathered[1][s], 16 * J * ((turn + w + 1) if s == 0 else (turn + 1)))
                        for k in range(4):
                            dve.wait_ge(z_up, 4 * q + k + 1)
                            nc.vector.tensor_tensor(
                                pre[:, 2 * k:2 * k + 2, :],
                                ps[:, 4 + k % 2, :].rearrange("p (j f) -> p j f", j=2),
                                gat[:, s, 4 * k * F:4 * (k + 1) * F].rearrange("p (j f) -> p j f", j=2),
                                ALU.add).then_inc(pre_up, 1)
                        for h in range(2):
                            dve.wait_ge(acts, 2 * q + h + 1)
                            nc.vector.tensor_tensor(msg[:, 0, 512 * h:512 * (h + 1)],
                                                    pos[:, 4 * h:4 * h + 4, :].rearrange("p j f -> p (j f)"),
                                                    sig[:, 4 * h:4 * h + 4, :].rearrange("p j f -> p (j f)"),
                                                    ALU.mult).then_inc(m_up, 1)
                        nxt = (s + 1) % U
                        dve.wait_ge(sum_free, q + 1)
                        front(w, U * i + s + 1, nxt, q + w + 1, (turn + w + 1) if nxt == 0 else turn)

            for n in range(FIN):
                s = n % U
                dve.wait_ge(fin_in[s], 16 * K * (n // U + 1))
                nc.vector.tensor_tensor(gat[:, s, 0:FW], gat[:, s, 0:FW], gat[:, s, FW:2 * FW],
                                        ALU.add).then_inc(fin_dve, 1)
                dve.wait_ge(fin_dve, n + 1)
                dve.wait_ge(fin_pool, n + 1)
                nc.vector.tensor_tensor(gat[:, s, 0:FW], gat[:, s, 0:FW], gat[:, s, 2 * FW:3 * FW],
                                        ALU.add).then_inc(fin_sum, 1)


_INS = ["x", "src", "dst", "edge_attr_128", "L0_gnn_W", "L0_gnn_a", "L1_gnn_W_weight", "L1_gnn_b_weight",
        "L1_gnn_W_gate", "L1_gnn_b_gate"]


def kernel(**inputs):
    import numpy as _np
    import concourse.bacc as _bacc
    from concourse import mybir as _mybir
    from concourse.bass_utils import run_bass_kernel_spmd as _run

    nc = _bacc.Bacc("TRN2", target_bir_lowering=False, num_devices=1)
    arrays, args = {}, []
    for name in _INS:
        v = _np.ascontiguousarray(inputs[name])
        arrays[f"in_{name}"] = v
        args.append(nc.dram_tensor(f"in_{name}", v.shape, _mybir.dt.from_np(v.dtype), kind="ExternalInput").ap())
    shape = arrays["in_x"].shape
    args.append(nc.dram_tensor("out_x", shape, _mybir.dt.float32, kind="ExternalOutput").ap())
    gnn_kernel(nc, *args)
    r = _run(nc, [arrays], core_ids=[0])
    return r.results[0]["out_x"]
```

```python
from contextlib import ExitStack

import concourse.bass as bass
from concourse import mybir

P = 128
F = 128
HEADS, HD = 4, 32
J = 8
GE = J * P
U = 4
C = 4
PN = 125
NT = C * PN
TW = F + HEADS
XU = 4
K = 4
FW = 500
EPS = 1e-5
SLOPE = 0.2
BIG = 32768.0

ALU = mybir.AluOpType
ACT = mybir.ActivationFunctionType
AX = mybir.AxisListType
F32 = mybir.dt.float32
BF16 = mybir.dt.bfloat16
I32 = mybir.dt.int32


def gnn_kernel(nc, x, src, dst, edge_attr, W, a, W_weight, b_weight, W_gate, b_gate, out):
    N, E = x.shape[0], src.shape[0]
    G = -(-E // (GE * U)) * U
    PAD = N + P
    FULL, REST = E // GE, E % GE
    CH = [(k, min(P, G + 1 - k)) for k in range(0, G + 1, P)]
    PADDED = [k for k, (g0, n) in enumerate(CH) if g0 + n > FULL]
    T = N // NT
    WINDOWS = -(-N // P)
    GU = G // U
    ZR = -(-N // GU)
    assert ZR * GU <= N + P and T // XU >= 2
    FIN = N // FW
    assert N % NT == 0 and T % XU == 1 and PAD < BIG and N % FW == 0
    assert GU >= 2 and FULL >= G - U and len(CH) <= 2 and K * FW <= 2 * GE and J % K == 0
    assert K == U and XU % 2 == 0 and T % 2 == 1

    with ExitStack() as ctx:
        def sb(name, shape, dt=F32):
            return ctx.enter_context(nc.sbuf_tensor(name, shape, dt))

        def sem(name):
            return ctx.enter_context(nc.semaphore(name))

        def sems(name, n):
            return [sem(f"{name}{i}") for i in range(n)]

        def dram(name, shape, dt=F32):
            return nc.dram_tensor(name, shape, dt, kind="Internal").ap()

        table0 = dram("table0", [N, TW])
        score_dst = dram("score_dst", [N + P, HEADS])
        x1 = [dram(f"x1_{k}", [N + P, F]) for k in range(2)]
        table_a = dram("table_a", [N, 2 * F])
        table_b = dram("table_b", [N + P, 2 * F])
        acc = [dram(f"acc{k}", [N + P, F]) for k in range(K)]
        pairs = dram("pairs", [G + 1, P, 2 * J], I32)
        digits = dram("digits", [G + 1, 2, 2 * GE], BF16)

        iota_n = sb("iota_n", [P, P])
        iota_p = sb("iota_p", [P, 1])
        dump = sb("dump", [P, 1])
        ident = sb("ident", [P, P])
        ident_b = sb("ident_b", [P, P], BF16)
        later_b = sb("later_b", [P, 4, P], BF16)
        ones = sb("ones", [P, P])
        ones_b = sb("ones_b", [2, P], BF16)
        zeros = sb("zeros", [P, max(NT, ZR)])
        eps = sb("eps", [P, 1])
        w0 = sb("w0", [P, F])
        a_diag = sb("a_diag", [P, 2 * HEADS])
        w0t = sb("w0t", [P, TW + HEADS])
        w_nodes = sb("w_nodes", [P, 4 * F])
        w_edge = sb("w_edge", [P, 2 * F])
        bias_row = sb("bias_row", [1, 2 * F])
        bias = sb("bias", [P, 2 * F])
        ends = sb("ends", [P, 4])
        diag = sb("diag", [P, 4, P])
        base = sb("base", [P, G + 1])
        span = sb("span", [P, G + 1])
        start = sb("start", [P, G + 1])
        span_max = sb("span_max", [P, 1])
        passes_i = sb("passes_i", [P, 3], I32)
        win = sb("win", [P, G + 1])
        win_i = sb("win_i", [P, G + 1], I32)
        node_id = sb("node_id", [P, G + 1])
        xt = sb("xt", [P, XU, C, F])
        xb = sb("xb", [P, XU, C, F])
        stats = sb("stats", [P, XU, C, 6])
        mv = sb("mv", [P, XU, C, 2])
        std = sb("std", [P, XU, C])
        rstd = sb("rstd", [P, XU, C])
        xn = sb("xn", [P, XU, C, F])
        ht = sb("ht", [P, 2, NT])
        t0 = sb("t0", [P, XU, C, TW])
        sd0 = sb("sd0", [P, XU, C, HEADS])
        idx = sb("idx", [P, U, 2 * J], I32)
        rows = sb("rows", [2, U, 2 * GE], BF16)
        sdw = sb("sdw", [P, U, HEADS])
        bw = sb("bw", [P, U, 2 * F])
        ea = sb("ea", [P, U, J * F])
        gat = sb("gat", [P, U, J * 2 * F])
        rel = sb("rel", [P, J])
        above = sb("above", [P, J])
        srcf = sb("srcf", [P, J])
        count = sb("count", [P, J])
        first = sb("first", [P, J])
        shift = sb("shift", [P, J])
        mask = sb("mask", [P, 2, J])
        sidx = sb("sidx", [P, U, J], I32)
        lin = sb("lin", [P, J, HEADS])
        att = sb("att", [P, J, HEADS])
        to_edge = sb("to_edge", [P, 2, GE])
        to_node = sb("to_node", [P, 2, GE])
        msg = sb("msg", [P, 2, GE])
        summed = sb("summed", [P, 2, GE])
        x1w = sb("x1w", [P, 2, F])
        x1o = sb("x1o", [P, 2, F])
        eat = sb("eat", [P, 2, 4 * P])
        pre = sb("pre", [P, J, 2 * F])
        sig = sb("sig", [P, J, F])
        pos = sb("pos", [P, J, F])
        same = to_node

        ps = ctx.enter_context(nc.psum_tensor("ps", [P, 8, 512], F32))
        bc_dst = ps[:, 0:2, :]
        bc_src = ps[:, 2:4, :]
        tp = ps[:, 6, :]
        mm = ps[:, 7, :]

        ab = gat[:].rearrange("p s (h c f) -> p s h c f", h=2, c=C)

        def prep_int(k):
            return gat[:, k, :].bitcast(I32).rearrange("p (s e) -> p s e", s=2)

        def prep_pairs(k):
            return ea[:, 2 * k:2 * k + 2, :].rearrange("p a b -> p (a b)").bitcast(I32)

        def prep_digits(k):
            return gat[:, 2 + k, :].bitcast(BF16)

        prep_low = pos[:].rearrange("p a b -> p (a b)").bitcast(I32)
        prep_high = sig[:].rearrange("p a b -> p (a b)").bitcast(I32)
        prep_real = msg[:, 0, :]

        consts, weights, w_ps, w_sb = sem("consts"), sem("weights"), sem("w_ps"), sem("w_sb")
        edges_in = sem("edges_in")
        prep_dve, prep_packed, prep_diag, prep_ps = (
            sem("prep_dve"), sem("prep_packed"), sem("prep_diag"), sem("prep_ps"))
        windows_known = sem("windows_known")
        stored, x1_zero, zeroed = sem("stored"), sem("x1_zero"), sem("zeroed")
        x_in, xb_in = sems("x_in", XU), sems("xb_in", XU)
        x_stored, t_stored = sems("x_stored", XU), sems("t_stored", XU)
        node_sum, node_dve, node_xn = sem("node_sum"), sem("node_dve"), sem("node_xn")
        node_var, node_std = sem("node_var"), sem("node_std")
        node_tp, node_ht, node_ps, half_up = sem("node_tp"), sem("node_ht"), sem("node_ps"), sem("half_up")
        node_out = sem("node_out")
        a_first, a_second, b_first, b_second = sem("a_first"), sem("a_second"), sem("b_first"), sem("b_second")
        nodes_done = sem("nodes_done")
        past_waits = sem("past_waits")
        pass_dve = sem("pass_dve")
        pass_go, pass_done = sems("pass_go", 2), sems("pass_done", 2)
        idx_in = [sems(f"idx_in{l}_", U) for l in range(2)]
        rows_in = [sems(f"rows_in{l}_", U) for l in range(2)]
        gathered = [sems(f"gathered{l}_", U) for l in range(2)]
        sdw_in, bw_in, ea_in = sems("sdw_in", U), sems("bw_in", U), sems("ea_in", U)
        bc0, to_edge0, dve0, expanded = sem("bc0"), sem("to_edge0"), sem("dve0"), sem("expanded")
        msgs0 = sem("msgs0")
        acc_up = sem("acc_up")
        copied0 = sem("copied0")
        x1_in, x1_st = sems("x1_in", 2), sems("x1_st", 2)
        bc1, to_edge1, dve1, same1, sidx_up = sem("bc1"), sem("to_edge1"), sem("dve1"), sem("same1"), sem("sidx_up")
        ea_tp, ea_t, z_up = sem("ea_tp"), sem("ea_t"), sem("z_up")
        pre_up = sem("pre_up")
        acts = sem("acts")
        m_up = sem("m_up")
        s_up, sum_up = sem("s_up"), sem("sum_up")
        sum_free = sem("sum_free")
        added = sems("added", K)
        fin_in, fin_out = sems("fin_in", U), sems("fin_out", U)
        fin_pool, fin_dve, fin_sum = sem("fin_pool"), sem("fin_dve"), sem("fin_sum")

        N_PADS, N_CONST = 1 + 2 * len(PADDED), 12 + 2 * len(PADDED)
        N_WEIGHT = 16 * (1 + 2 * HEADS + 6 + 2)
        N_STORED = 16 * 2 * len(CH)
        FRONT = 7
        STEPS0 = 4

        def node_rows(table, t):
            return table[bass.ds(t * NT, NT), :].rearrange("(p c) f -> p (c f)", c=C)

        def slot_rounds(s, layer):
            return layer * (T // XU + (1 if s == 0 else 0))

        block = ctx.enter_context(nc.Block())

        @block.sync
        def _(sp):
            sp.wait_ge(consts, N_PADS)
            for k, (g0, n) in enumerate(CH):
                full = max(0, min(n, FULL - g0))
                for s, arr in enumerate((src, dst)):
                    if full:
                        sp.dma_start(prep_int(k)[0:full, s, :], arr[g0 * GE:(g0 + full) * GE].rearrange(
                            "(g e) -> g e", e=GE)).then_inc(edges_in, 16)
                    else:
                        sp.sem_inc(edges_in, 16)
                    if REST and g0 <= FULL < g0 + n:
                        sp.dma_start(prep_int(k)[full:full + 1, s, 0:REST],
                                     arr[FULL * GE:E].rearrange("(g e) -> g e", g=1)).then_inc(edges_in, 16)
                    else:
                        sp.sem_inc(edges_in, 16)
            sp.dma_start(w0[:], W).then_inc(weights, 16)
            for h in range(HEADS):
                for i in range(2):
                    sp.dma_start(a_diag[h * HD:(h + 1) * HD, i * HEADS + h:i * HEADS + h + 1],
                                 a[h:h + 1, i * HD:(i + 1) * HD].rearrange("o d -> d o")).then_inc(weights, 16)
            for i, w in enumerate((W_weight, W_gate)):
                sp.dma_start(w_nodes[:, i * F:(i + 1) * F], w[0:F, :]).then_inc(weights, 16)
                sp.dma_start(w_nodes[:, (2 + i) * F:(3 + i) * F], w[F:2 * F, :]).then_inc(weights, 16)
                sp.dma_start(w_edge[:, i * F:(i + 1) * F], w[2 * F:3 * F, :]).then_inc(weights, 16)
            for i, b in enumerate((b_weight, b_gate)):
                sp.dma_start(bias_row[:, i * F:(i + 1) * F], b.rearrange("(o f) -> o f", o=1)).then_inc(weights, 16)
            for k, (g0, n) in enumerate(CH):
                sp.wait_ge(prep_packed, k + 1)
                sp.dma_start(pairs[g0:g0 + n].rearrange("g p s -> g (p s)"), prep_pairs(k)[0:n, :]).then_inc(stored, 16)
                sp.dma_start(digits[g0:g0 + n].rearrange("g d e -> g (d e)"),
                             prep_digits(k)[0:n, :]).then_inc(stored, 16)

            def load_nodes(layer, t, i, s):
                sp.wait_ge(x_stored[s], 16 * (i + slot_rounds(s, layer) + 1))
                sp.dma_start(xt[0:PN, s].rearrange("p c f -> p (c f)"),
                             node_rows(x1[0] if layer else x, t)).then_inc(x_in[s], 16)
                if layer == 1:
                    sp.dma_start(xb[0:PN, s].rearrange("p c f -> p (c f)"),
                                 node_rows(x1[1], t)).then_inc(xb_in[s], 16)

            def load_front(layer, g, s, pads=False):
                sp.dma_start(rows[:, s, :], digits[bass.ds(g, 1)].rearrange(
                    "g d e -> (g d) e")).then_inc(rows_in[layer][s], 16)
                if layer == 1 or not pads:
                    sp.dma_start(idx[:, s, :], pairs[bass.ds(g, 1)].rearrange(
                        "g p s -> (g p) s")).then_inc(idx_in[layer][s], 16)

            def load_window(layer, g, s):
                start = sp.value_load(win_i[0:1, bass.ds(g, 1)], min_val=0, max_val=N)
                if layer == 0:
                    sp.dma_start(sdw[:, s, :], score_dst[bass.ds(start, P), :]).then_inc(sdw_in[s], 16)
                else:
                    sp.dma_start(bw[:, s, :], table_b[bass.ds(start, P), :]).then_inc(bw_in[s], 16)

            def load_edges(g, s, n):
                whole, part = n // J, n % J
                if n == GE:
                    whole, part = P // 2, J
                last = whole + (P // 2 if n == GE else 1)
                rows_of = edge_attr[bass.ds(g * GE, n), :] if n else None
                if whole:
                    sp.dma_start(ea[0:whole, s, :], rows_of[0:whole * J, :].rearrange(
                        "(p j) f -> p (j f)", j=J)).then_inc(ea_in[s], 16)
                else:
                    sp.sem_inc(ea_in[s], 16)
                if part:
                    sp.dma_start(ea[whole:last, s, 0:part * F], rows_of[whole * J:n, :].rearrange(
                        "(p j) f -> p (j f)", j=part)).then_inc(ea_in[s], 16)
                else:
                    sp.sem_inc(ea_in[s], 16)

            def edge_loads(layer, passes):
                free = msgs0 if layer == 0 else m_up
                per = 1 if layer == 0 else 2
                with sp.Fori(0, passes) as w:
                    sp.wait_ge(pass_go[layer], w + 1)
                    sp.sem_inc(past_waits, 1)
                    with sp.Fori(0, GU - layer) as i:
                        for s in range(U):
                            sp.wait_ge(free, per * (U * (w * GU + i) + s + 1))
                            load_front(layer, U * i + s, s)
                            load_window(layer, U * i + s, s)
                            if layer == 1:
                                load_edges(U * i + s, s, GE)
                    if layer == 1:
                        for s in range(U):
                            g = G - U + s
                            sp.wait_ge(free, per * (w * G + g + 1))
                            load_front(layer, g, s)
                            load_window(layer, g, s)
                            load_edges(g, s, GE if g < FULL else REST if g == FULL else 0)
                    sp.wait_ge(free, per * (w * G + G + 1))
                    load_front(layer, G, 0, pads=True)

            for layer in range(2):
                if layer == 1:
                    sp.wait_ge(pass_done[0], 2 * passes + 1)
                    sp.sem_inc(past_waits, 1)
                with sp.Fori(0, T // XU) as i:
                    for s in range(XU):
                        load_nodes(layer, XU * i + s, i, s)
                load_nodes(layer, T - 1, T // XU, 0)
                if layer == 0:
                    sp.wait_ge(windows_known, 1)
                    passes = sp.value_load(passes_i[0:1, 2:3], min_val=1, max_val=WINDOWS)
                sp.wait_ge(nodes_done, layer + 1)
                edge_loads(layer, passes)

            sp.wait_ge(pass_done[1], passes + 1)
            for n in range(FIN):
                if n >= U:
                    sp.wait_ge(fin_out[n % U], 16 * (n // U))
                for k in range(K):
                    flat = acc[k][0:N, :].rearrange("n f -> (n f)").rearrange("(p e) -> p e", p=P)
                    sp.dma_start(gat[:, n % U, k * FW:(k + 1) * FW],
                                 flat[:, n * FW:(n + 1) * FW]).then_inc(fin_in[n % U], 16)

        @block.gpsimd
        def _(pool):
            pool.sem_inc(pass_done[1], 1)
            step = [0]

            def const(ins):
                step[0] += 1
                ins.then_inc(consts, 1)
                pool.wait_ge(consts, step[0])

            const(nc.gpsimd.memset(a_diag[:], 0.0))
            for k in PADDED:
                const(nc.gpsimd.memset(gat[:, k, 0:GE].bitcast(I32), 0))
                const(nc.gpsimd.memset(gat[:, k, GE:2 * GE].bitcast(I32), PAD))
            const(nc.gpsimd.memset(ones[:], 1.0))
            const(nc.gpsimd.memset(ones_b[:], 1.0))
            const(nc.gpsimd.memset(eps[:], EPS))
            const(nc.gpsimd.iota(iota_n[:], [[1, P]], base=0, channel_multiplier=0,
                                 allow_small_or_imprecise_dtypes=True))
            const(nc.gpsimd.iota(iota_p[:], [[0, 1]], base=0, channel_multiplier=1,
                                 allow_small_or_imprecise_dtypes=True))
            const(nc.gpsimd.affine_select(out=ident[:], in_=ones[:], pattern=[[-1, P]], compare_op=ALU.is_equal,
                                          fill=0.0, base=0, channel_multiplier=1))
            const(nc.gpsimd.memset(later_b[:], BIG))
            const(nc.gpsimd.affine_select(out=later_b[:], in_=later_b[:], pattern=[[0, 4], [1, P]],
                                          compare_op=ALU.is_gt, fill=0.0, base=0, channel_multiplier=-1))
            const(nc.gpsimd.iota(dump[:], [[0, 1]], base=N, channel_multiplier=1,
                                 allow_small_or_imprecise_dtypes=True))
            const(nc.gpsimd.tensor_copy(ident_b[:], ident[:]))
            const(nc.gpsimd.memset(zeros[:], 0.0))
            assert step[0] == N_CONST
            for k in range(K):
                pool.dma_start(acc[k][N:N + P, :], zeros[:, 0:F]).then_inc(added[k], 16)
            for s in range(XU):
                at = N + P // XU * s
                for table, width, done in ((x1[0], F, x_stored), (score_dst, HEADS, t_stored),
                                           (table_b, 2 * F, t_stored)):
                    pool.dma_start(table[at:at + P // XU, :], zeros[0:P // XU, 0:width]).then_inc(done[s], 16)

            def store_x(layer, t, s):
                n = t + layer * T
                pool.wait_ge(node_xn, n + 1)
                pool.sem_inc(past_waits, 1)
                pool.dma_start(node_rows(acc[0] if layer else x1[0], t),
                               xt[0:PN, s].rearrange("p c f -> p (c f)")).then_inc(x_stored[s], 16)

            def store_outs(layer, t, s):
                if layer == 0:
                    pool.wait_ge(node_out, t + 2)
                    pool.sem_inc(past_waits, 1)
                    pool.dma_start(node_rows(table0, t),
                                   t0[0:PN, s].rearrange("p c f -> p (c f)")).then_inc(t_stored[s], 16)
                    pool.dma_start(node_rows(score_dst, t),
                                   sd0[0:PN, s].rearrange("p c f -> p (c f)")).then_inc(t_stored[s], 16)
                else:
                    pool.wait_ge(b_second, 2 * t + 4)
                    pool.sem_inc(past_waits, 1)
                    pool.dma_start(node_rows(table_b, t),
                                   ab[0:PN, s, 1].rearrange("p c f -> p (c f)")).then_inc(t_stored[s], 16)
                    pool.wait_ge(a_second, 2 * t + 4)
                    pool.sem_inc(past_waits, 1)
                    pool.dma_start(node_rows(table_a, t),
                                   ab[0:PN, s, 0].rearrange("p c f -> p (c f)")).then_inc(t_stored[s], 16)

            def gather(layer, s, table, width):
                pool.sem_inc(past_waits, 1)
                for j in range(J):
                    nc.gpsimd.indirect_dma_start(
                        out=gat[:, s, j * width:(j + 1) * width], out_offset=None, in_=table,
                        in_offset=bass.IndirectOffsetOnAxis(ap=idx[:, s, j:j + 1], axis=0),
                    ).then_inc(gathered[layer][s], 16)

            for layer in range(2):
                store_x(layer, 0, 0)
                store_x(layer, 1, 1)
                with pool.Fori(0, T // XU - 1) as i:
                    for s in range(XU):
                        store_x(layer, XU * i + s + 2, (s + 2) % XU)
                        store_outs(layer, XU * i + s, s)
                for t in range(T - 1 - XU, T):
                    if t + 2 < T:
                        store_x(layer, t + 2, (t + 2) % XU)
                    store_outs(layer, t, t % XU)
                for s in range(XU):
                    pool.wait_ge(x_stored[s], 16 * (slot_rounds(s, layer + 1) + 1))
                    pool.wait_ge(t_stored[s], 32 * (slot_rounds(s, layer + 1) + 1))
                if layer == 0:
                    pool.wait_ge(stored, N_STORED)
                    pool.wait_ge(windows_known, 1)
                    passes = pool.value_load(passes_i[0:1, 2:3], min_val=1, max_val=WINDOWS)
                else:
                    pool.wait_ge(zeroed, 16 * (K - 1) * GU * passes)
                pool.sem_inc(nodes_done, 1)

                if layer == 0:
                    with pool.Fori(0, passes) as w:
                        with pool.Fori(0, GU) as i:
                            turn = pool.snap(w * GU + i)
                            for s in range(U):
                                pool.wait_ge(msgs0, U * turn + s + 1)
                                pool.wait_ge(idx_in[0][s], 16 * (turn + 1))
                                gather(0, s, table0, TW)
                    continue

                with pool.Fori(0, passes) as w:
                    pool.wait_ge(pass_go[1], w + 1)
                    pool.wait_ge(idx_in[1][0], 16 * (w * GU + w + 1))
                    gather(1, 0, table_a, 2 * F)
                    with pool.Fori(0, GU) as i:
                        turn = pool.snap(w * GU + i)
                        for s in range(U):
                            q = U * turn + s
                            nxt = (s + 1) % U
                            pool.wait_ge(m_up, 2 * (q + 2))
                            pool.wait_ge(idx_in[1][nxt], 16 * ((turn + w + 2) if nxt == 0 else (turn + 1)))
                            gather(1, nxt, table_a, 2 * F)
                            pool.wait_ge(sidx_up, q + w + 1)
                            for j in range(J):
                                if j % (J // 2) == 0:
                                    pool.wait_ge(sum_up, 2 * q + j // (J // 2) + 2)
                                pool.wait_ge(added[j % K], 16 * ((J // K) * q + j // K + 1))
                                if j == K:
                                    pool.sem_inc(sum_free, 1)
                                else:
                                    pool.sem_inc(past_waits, 1)
                                nc.gpsimd.indirect_dma_start(
                                    out=acc[j % K], out_offset=bass.IndirectOffsetOnAxis(
                                        ap=sidx[:, s, j:j + 1], axis=0),
                                    in_=summed[:, s % 2, j * F:(j + 1) * F], in_offset=None,
                                    bounds_check=N + P - 1, oob_is_err=True,
                                    compute_op=ALU.add).then_inc(added[j % K], 16)
                    for k in range(K):
                        pool.wait_ge(added[k], 16 * ((J // K) * (w * G + G) + 1))
                    pool.wait_ge(gathered[1][0], 16 * J * (w * GU + GU + w + 1))
                    pool.sem_inc(pass_done[1], 1)

            for n in range(FIN):
                s = n % U
                pool.wait_ge(fin_in[s], 16 * K * (n // U + 1))
                nc.gpsimd.tensor_tensor(gat[:, s, 2 * FW:3 * FW], gat[:, s, 2 * FW:3 * FW],
                                        gat[:, s, 3 * FW:4 * FW], ALU.add).then_inc(fin_pool, 1)

        @block.tensor
        def _(pe):
            pe.sem_inc(acc_up, 2)
            pe.wait_ge(consts, N_CONST)
            pe.wait_ge(weights, N_WEIGHT)
            pe.transpose(ps[:, 0, 0:F], w0[:], ident[:])
            pe.matmul(ps[:, 1, 0:2 * HEADS], w0[:], a_diag[:], start=True, stop=True)
            pe.matmul(ps[:, 2, 0:2 * F], ones[0:1, :], bias_row[:], start=True, stop=True).then_inc(w_ps, 1)
            pe.wait_ge(prep_diag, 1)
            for c in range(4):
                mmi = pe.matmul(ps[:, 4 + c // 2, (c % 2) * P:(c % 2) * P + P], ones[:], diag[:, c, :],
                                start=True, stop=True)
            mmi.then_inc(prep_ps, 1)
            pe.wait_ge(w_sb, 3)

            def node_turned(layer, t, s):
                n = t + layer * T
                if layer or not isinstance(t, int) or t > 0:
                    pe.wait_ge(node_ht, n)
                pe.wait_ge(node_xn, n + 1)
                for c in range(C):
                    mmi = pe.transpose(tp[:, c * PN:(c + 1) * PN], xn[0:PN, s, c, :], ident[0:PN, 0:PN])
                mmi.then_inc(node_tp, 1)

            def node_products(layer, t, s):
                n = t + layer * T
                pe.wait_ge(node_ht, n + 1)
                if layer == 0:
                    pe.wait_ge(node_out, t + 1)
                wt, width = (w0t, TW + HEADS) if layer == 0 else (w_nodes, 4 * F)
                for c in range(C):
                    if layer == 1 and c % 2 == 0:
                        pe.wait_ge(a_second, 2 * t + c // 2 + 1)
                        pe.wait_ge(b_second, 2 * t + c // 2 + 1)
                    mmi = pe.matmul(ps[0:PN, c, 0:width], ht[:, s % 2, c * PN:(c + 1) * PN], wt[:, 0:width],
                                    start=True, stop=True)
                    if layer == 1 and c % 2 == 1:
                        mmi.then_inc(half_up, 1)
                if layer == 0:
                    mmi.then_inc(node_ps, 1)

            def nodes(layer):
                def step(t, s):
                    node_turned(layer, t + 1, (s + 1) % XU)
                    node_products(layer, t, s)

                node_turned(layer, 0, 0)
                with pe.Fori(0, T // XU) as i:
                    for s in range(XU):
                        step(XU * i + s, s)
                node_products(layer, T - 1, 0)

            nodes(0)
            pe.wait_ge(node_out, T + 1)
            pe.wait_ge(windows_known, 1)
            passes = pe.value_load(passes_i[0:1, 2:3], min_val=1, max_val=WINDOWS)

            def spread_dst0(s, f, q):
                pe.wait_ge(rows_in[0][s], f)
                pe.wait_ge(to_edge0, q + 1)
                for b in range(2):
                    mmi = pe.matmul(bc_dst[:, b, :], ones_b[:], rows[:, s, GE + 512 * b:GE + 512 * (b + 1)],
                                    start=True, stop=True)
                mmi.then_inc(bc0, 1)

            with pe.Fori(0, passes) as w:
                spread_dst0(0, 16 * (w * GU + w + 1), w * G)
                with pe.Fori(0, GU) as i:
                    turn = pe.snap(w * GU + i)
                    for s in range(U):
                        q = U * turn + s
                        pe.wait_ge(to_edge0, q + 2)
                        pe.wait_ge(sdw_in[s], 16 * (turn + 1))
                        for j in range(J):
                            mmi = pe.matmul(ps[:, 6 + s % 2, j * HEADS:(j + 1) * HEADS],
                                            to_edge[:, 0, j * P:(j + 1) * P], sdw[:, s, :], start=True, stop=True)
                        mmi.then_inc(expanded, 1)
                        nxt = (s + 1) % U
                        spread_dst0(nxt, 16 * ((turn + w + 2) if nxt == 0 else (turn + 1)), q + 1)
                        pe.wait_ge(x1_in[s % 2], 16 * (2 * turn + s // 2 + 1 + (w if s % 2 == 0 else 0)))
                        pe.wait_ge(copied0, q + 1)
                        pe.wait_ge(msgs0, q + 1 + U)
                        out_ps = ps[:, 4 + s % 2, 0:F]
                        pe.matmul(out_ps, ident[:], x1w[:, s % 2, :], start=True, stop=False)
                        for j in range(J):
                            mmi = pe.matmul(out_ps, to_node[:, s % 2, j * P:(j + 1) * P],
                                            msg[:, s % 2, j * F:(j + 1) * F], start=False, stop=(j == J - 1))
                        mmi.then_inc(acc_up, 1)
                pe.wait_ge(bc0, w * G + G + w + 1)
                pe.sem_inc(pass_done[0], 1)

            nodes(1)
            pe.wait_ge(a_second, 2 * T + 2)
            pe.wait_ge(b_second, 2 * T + 2)

            def spread1(s, f, done):
                pe.wait_ge(rows_in[1][s], f)
                pe.wait_ge(same1, done + 1)
                for b in range(2):
                    mmi = pe.matmul(bc_dst[:, b, :], ones_b[:], rows[:, s, GE + 512 * b:GE + 512 * (b + 1)],
                                    start=True, stop=True)
                mmi.then_inc(bc1, 1)
                for b in range(2):
                    pe.matmul(bc_src[:, b, :], ones_b[:], rows[:, s, 512 * b:512 * (b + 1)], start=True, stop=False)
                    mmi = pe.matmul(bc_src[:, b, :], ident_b[:], later_b[:].rearrange("p t n -> p (t n)"),
                                    start=False, stop=True)
                mmi.then_inc(bc1, 1)

            with pe.Fori(0, passes) as w:
                spread1(0, 16 * (w * GU + w + 1), w * G + w)
                with pe.Fori(0, GU) as i:
                    turn = pe.snap(w * GU + i)
                    for s in range(U):
                        q = U * turn + s
                        pe.wait_ge(ea_in[s], 32 * (turn + 1))
                        for h in range(2):
                            pe.wait_ge(ea_t, 2 * q + h + 1)
                            for j in range(4 * h, 4 * h + 4):
                                mmi = pe.transpose(tp[:, (j % 4) * P:(j % 4 + 1) * P],
                                                   ea[:, s, j * F:(j + 1) * F], ident[:])
                            mmi.then_inc(ea_tp, 1)
                        pe.wait_ge(to_edge1, q + w + 1)
                        pe.wait_ge(bw_in[s], 16 * (turn + 1))
                        for k in range(4):
                            if k % 2 == 0:
                                pe.wait_ge(ea_t, 2 * q + k // 2 + 2)
                            pe.wait_ge(pre_up, 4 * q + k + 1)
                            for j in range(2 * k, 2 * k + 2):
                                z = ps[:, 4 + k % 2, (j % 2) * 2 * F:(j % 2 + 1) * 2 * F]
                                pe.matmul(z, eat[:, j // 4, (j % 4) * P:(j % 4 + 1) * P], w_edge[:],
                                          start=True, stop=False)
                                mmi = pe.matmul(z, to_edge[:, s % 2, j * P:(j + 1) * P], bw[:, s, :],
                                                start=False, stop=True)
                            mmi.then_inc(z_up, 1)
                        nxt = (s + 1) % U
                        spread1(nxt, 16 * ((turn + w + 2) if nxt == 0 else (turn + 1)), q + w + 1)
                        for h in range(2):
                            pe.wait_ge(m_up, 2 * U + 2 * q + h + 1)
                            pe.wait_ge(sum_up, 2 * q + h + 1)
                            for j in range(4 * h, 4 * h + 4):
                                mmi = pe.matmul(mm[:, (j % 4) * F:(j % 4 + 1) * F],
                                                same[:, s % 2, j * P:(j + 1) * P],
                                                msg[:, 0, j * F:(j + 1) * F], start=True, stop=True)
                            mmi.then_inc(s_up, 1)

        @block.scalar
        def _(act):
            act.sem_inc(copied0, 2)
            act.sem_inc(pass_done[0], 1)
            for one in (ea_t, sum_up, node_out):
                act.sem_inc(one, 1)
            act.sem_inc(a_second, 2)
            act.wait_ge(consts, N_CONST)
            for k in range(2):
                at = N + P // 2 * k
                act.dma_start(x1[1][at:at + P // 2, :], zeros[0:P // 2, 0:F]).then_inc(x1_st[k], 16)
            def root(n, s):
                act.wait_ge(node_var, n + 1)
                nc.scalar.activation(std[0:PN, s, :], mv[0:PN, s, :, 1], ACT.Sqrt,
                                     bias=eps[0:PN, :]).then_inc(node_std, 1)

            def relu_out(layer, t, s):
                act.wait_ge(node_tp, t + layer * T + 1)
                nc.scalar.activation(ht[:, s % 2], tp[:, 0:NT], ACT.Relu).then_inc(node_ht, 1)

            def outs(layer, t, i, s):
                act.wait_ge(t_stored[s], 32 * (i + slot_rounds(s, layer) + 1))
                if layer == 0:
                    act.wait_ge(node_ps, t + 1)
                    nc.scalar.activation(t0[0:PN, s], ps[0:PN, 0:C, 0:TW], ACT.Copy)
                    nc.scalar.activation(sd0[0:PN, s], ps[0:PN, 0:C, TW:TW + HEADS], ACT.Copy).then_inc(node_out, 1)
                    return
                for h in range(2):
                    act.wait_ge(half_up, 2 * t + h + 1)
                    nc.scalar.activation(ab[0:PN, s, 0, 2 * h], ps[0:PN, 2 * h, 0:2 * F], ACT.Copy).then_inc(a_first, 1)
                    act.wait_ge(b_first, 2 * t + h + 1)
                    nc.scalar.activation(ab[0:PN, s, 0, 2 * h + 1], ps[0:PN, 2 * h + 1, 0:2 * F],
                                         ACT.Copy).then_inc(a_second, 1)

            def zero_rows(table, first, n):
                return act.dma_start(table[bass.ds(first, n), :].rearrange("n f -> (n f)").rearrange(
                    "(p e) -> p e", p=P), zeros[:, 0:n])

            def nodes(layer):
                def step(t, i, s, last=False):
                    relu_out(layer, t + 1, s + 1)
                    if not last:
                        root(t + 2 + layer * T, (s + 2) % XU)
                    if layer == 0:
                        zero_rows(x1[1], t * NT, NT).then_inc(x1_zero, 16)
                    outs(layer, t, i, s)

                root(layer * T, 0)
                root(layer * T + 1, 1)
                relu_out(layer, 0, 0)
                with act.Fori(0, T // XU - 1) as i:
                    for s in range(XU):
                        step(XU * i + s, i, s)
                for s in range(XU):
                    step(T - 1 - XU + s, T // XU - 1, s, last=s == XU - 1)
                if layer == 0:
                    zero_rows(x1[1], (T - 1) * NT, NT).then_inc(x1_zero, 16)
                outs(layer, T - 1, T // XU, 0)

            nodes(0)
            act.wait_ge(windows_known, 1)
            passes = act.value_load(passes_i[0:1, 2:3], min_val=1, max_val=WINDOWS)
            act.wait_ge(nodes_done, 1)
            act.wait_ge(x1_zero, 16 * T)
            for k in range(1, K):
                act.wait_ge(added[k], 16)
            with act.Fori(0, passes) as w:
                act.wait_ge(pass_go[0], w + 1)
                act.sem_inc(past_waits, 1)
                first = act.value_load(win_i[0:1, 0:1], min_val=0, max_val=N)
                act.wait_ge(x1_st[0], 16 * (w * (G // 2) + 1))
                act.dma_start(x1w[:, 0, :], x1[0][bass.ds(first, P), :]).then_inc(x1_in[0], 16)
                with act.Fori(0, GU) as i:
                    turn = act.snap(w * GU + i)
                    for s in range(U):
                        q = U * turn + s
                        start = act.value_load(win_i[0:1, bass.ds(U * i + s, 1)], min_val=0, max_val=N)
                        after = act.value_load(win_i[0:1, bass.ds(U * i + s + 1, 1)], min_val=0, max_val=N)
                        nxt = (s + 1) % 2
                        act.wait_ge(x1_st[nxt], 16 * (2 * turn + (s + 1) // 2 + 1))
                        act.dma_start(x1w[:, nxt, :], x1[nxt][bass.ds(after, P), :]).then_inc(x1_in[nxt], 16)
                        act.wait_ge(acc_up, q + 3)
                        nc.scalar.activation(x1o[:, s % 2, :], ps[:, 4 + s % 2, 0:F], ACT.Copy).then_inc(copied0, 1)
                        act.wait_ge(copied0, q + 3)
                        act.dma_start(x1[s % 2][bass.ds(start, P), :], x1o[:, s % 2, :]).then_inc(x1_st[s % 2], 16)
                        if s > 0:
                            zero_rows(acc[s], i * ZR, ZR).then_inc(zeroed, 16)
                act.wait_ge(x1_in[0], 16 * (w * (G // 2) + G // 2 + w + 1))
                for k in range(2):
                    act.wait_ge(x1_st[k], 16 * (w * (G // 2) + G // 2 + 1))
                act.wait_ge(zeroed, 16 * (K - 1) * GU * (w + 1))
                act.sem_inc(pass_done[0], 1)

            nodes(1)
            with act.Fori(0, passes) as w:
                with act.Fori(0, GU) as i:
                    turn = act.snap(w * GU + i)
                    for s in range(U):
                        q = U * turn + s
                        for h in range(2):
                            act.wait_ge(ea_tp, 2 * q + h + 1)
                            nc.scalar.activation(eat[:, h, :], tp, ACT.Copy).then_inc(ea_t, 1)
                        for h in range(2):
                            act.wait_ge(pre_up, 4 * q + 2 * (h + 1) + 2)
                            for j in range(4 * h, 4 * h + 4):
                                nc.scalar.activation(pos[:, j, :], pre[:, j, 0:F], ACT.Relu,
                                                     scale=mask[:, s % 2, j:j + 1])
                            nc.scalar.activation(sig[:, 4 * h:4 * h + 4, :], pre[:, 4 * h:4 * h + 4, F:2 * F],
                                                 ACT.Sigmoid).then_inc(acts, 1)
                        act.wait_ge(sum_free, q + 2)
                        for h in range(2):
                            act.wait_ge(s_up, 2 * q + h + 1)
                            nc.scalar.activation(summed[:, s % 2, 512 * h:512 * (h + 1)], mm,
                                                 ACT.Copy).then_inc(sum_up, 1)

            for n in range(FIN):
                flat = out.rearrange("n f -> (n f)").rearrange("(p e) -> p e", p=P)
                act.wait_ge(fin_sum, n + 1)
                act.dma_start(flat[:, n * FW:(n + 1) * FW], gat[:, n % U, 0:FW]).then_inc(fin_out[n % U], 16)
            for s in range(U):
                act.wait_ge(fin_out[s], 16 * len(range(s, FIN, U)))

        @block.vector
        def _(dve):
            dve.sem_inc(msgs0, U)
            dve.sem_inc(pre_up, 2)
            dve.sem_inc(m_up, 2 * U)
            dve.sem_inc(sum_free, 2)
            dve.sem_inc(b_second, 2)
            for one in (to_edge0, same1):
                dve.sem_inc(one, 1)
            step = [0]

            def link(ins):
                step[0] += 1
                ins.then_inc(prep_dve, 1)
                dve.wait_ge(prep_dve, step[0])

            dve.wait_ge(edges_in, 64 * len(CH))
            link(nc.vector.memset(ends[:], 0.0))
            for k, (g0, n) in enumerate(CH):
                for s in range(2):
                    e = prep_int(k)[:, s, :]
                    link(nc.vector.tensor_copy(
                        prep_pairs(k).rearrange("g (p s j) -> g p s j", s=2, j=J)[:, :, s, :],
                        e.rearrange("g (p j) -> g p j", j=J)))
                    link(nc.vector.tensor_scalar(prep_low, e, P - 1, None, ALU.bitwise_and))
                    link(nc.vector.tensor_tensor(prep_high, e, prep_low, ALU.subtract))
                    for d, digit in enumerate((prep_high, prep_low)):
                        link(nc.vector.tensor_copy(
                            prep_digits(k).rearrange("g (d s j p) -> g d s p j", d=2, s=2, j=J)[:, d, s],
                            digit.rearrange("g (p j) -> g p j", j=J)))
                dve.sem_inc(prep_packed, 1)
                e = prep_int(k)[:, 1, :]
                link(nc.vector.tensor_reduce(ends[:, k:k + 1], e, AX.X, ALU.min))
                link(nc.vector.scalar_tensor_tensor(prep_real, e, float(N), e, ALU.is_lt, ALU.mult))
                link(nc.vector.tensor_reduce(ends[:, 2 + k:3 + k], prep_real, AX.X, ALU.max))
            link(nc.vector.tensor_tensor(ends[:, 2:4], ends[:, 2:4], ends[:, 0:2], ALU.subtract))
            dve.wait_ge(consts, N_CONST)
            for c in range(4):
                link(nc.vector.tensor_scalar(diag[:, c, :], ident[:], ends[:, c:c + 1], None, ALU.mult))
            dve.sem_inc(prep_diag, 1)
            dve.wait_ge(w_ps, 1)
            nc.vector.tensor_copy(w0t[:, 0:F], ps[:, 0, 0:F]).then_inc(w_sb, 1)
            nc.vector.tensor_copy(w0t[:, F:TW + HEADS], ps[:, 1, 0:2 * HEADS]).then_inc(w_sb, 1)
            nc.vector.tensor_copy(bias[:], ps[:, 2, 0:2 * F]).then_inc(w_sb, 1)
            dve.wait_ge(prep_ps, 1)
            for k, (g0, n) in enumerate(CH):
                link(nc.vector.tensor_copy(base[:, g0:g0 + n], ps[:, 4, k * P:k * P + n]))
                link(nc.vector.tensor_copy(span[:, g0:g0 + n], ps[:, 5, k * P:k * P + n]))
            link(nc.vector.tensor_reduce(span_max[:], span[:], AX.X, ALU.max))
            link(nc.vector.tensor_copy(passes_i[:, 0:1], span_max[:]))
            link(nc.vector.tensor_scalar(passes_i[:, 1:2], passes_i[:, 0:1], 7, None, ALU.arith_shift_right))
            link(nc.vector.tensor_scalar(passes_i[:, 2:3], passes_i[:, 1:2], 1.0, None, ALU.add))
            dve.sem_inc(windows_known, 1)
            passes = dve.value_load(passes_i[0:1, 2:3], min_val=1, max_val=WINDOWS)

            def normalise(layer, t, i, s):
                n = t + layer * T
                dve.wait_ge(x_in[s], 16 * (i + slot_rounds(s, layer) + 1))
                if layer == 1:
                    dve.wait_ge(xb_in[s], 16 * (i + 1))
                    nc.vector.tensor_tensor(xt[0:PN, s], xt[0:PN, s], xb[0:PN, s], ALU.add).then_inc(node_sum, 1)
                    dve.wait_ge(node_sum, t + 1)
                for c in range(C):
                    ins = nc.vector.bn_stats(stats[0:PN, s, c, :], xt[0:PN, s, c, :])
                ins.then_inc(node_dve, 1)
                dve.wait_ge(node_dve, 2 * n + 1)
                dve.sem_inc(past_waits, 1)
                for c in range(C):
                    ins = nc.vector.bn_aggr(mv[0:PN, s, c, :], stats[0:PN, s, c, :])
                ins.then_inc(node_var, 1)
                dve.wait_ge(node_std, n + 1)
                nc.vector.reciprocal(rstd[0:PN, s, :], std[0:PN, s, :]).then_inc(node_dve, 1)
                dve.wait_ge(node_dve, 2 * n + 2)
                for c in range(C):
                    ins = nc.vector.tensor_scalar(xn[0:PN, s, c, :], xt[0:PN, s, c, :], mv[0:PN, s, c, 0:1],
                                                  rstd[0:PN, s, c:c + 1], ALU.subtract, ALU.mult)
                ins.then_inc(node_xn, 1)

            def node_outs(t, i, s):
                dve.wait_ge(t_stored[s], 32 * (i + slot_rounds(s, 1) + 1))
                for h in range(2):
                    dve.wait_ge(half_up, 2 * t + h + 1)
                    nc.vector.tensor_tensor(ab[0:PN, s, 1, 2 * h + 1], ps[0:PN, 2 * h + 1, 2 * F:4 * F], bias[0:PN, :],
                                            ALU.add).then_inc(b_first, 1)
                    dve.wait_ge(a_first, 2 * t + h + 1)
                    nc.vector.tensor_tensor(ab[0:PN, s, 1, 2 * h], ps[0:PN, 2 * h, 2 * F:4 * F], bias[0:PN, :],
                                            ALU.add).then_inc(b_second, 1)

            def nodes(layer):
                def step(i, s, last=False):
                    if not last:
                        normalise(layer, XU * i + s + 2, (i + 1) if s >= XU - 2 else i, (s + 2) % XU)
                    if layer == 1:
                        node_outs(XU * i + s, i, s)

                normalise(layer, 0, 0, 0)
                normalise(layer, 1, 0, 1)
                with dve.Fori(0, T // XU - 1) as i:
                    for s in range(XU):
                        step(i, s)
                for s in range(XU):
                    step(T // XU - 1, s, last=s == XU - 1)
                if layer == 1:
                    node_outs(T - 1, T // XU, 0)

            def windows(layer, w, steps):
                if layer == 0:
                    dve.wait_ge(pass_done[0], 2 * w + 1)
                else:
                    dve.wait_ge(pass_done[1], w + 1)
                nc.vector.tensor_scalar(win[:], start[:], float(N), None, ALU.min).then_inc(pass_dve, 1)
                dve.wait_ge(pass_dve, steps + 1)
                nc.vector.tensor_copy(win_i[:], win[:]).then_inc(pass_dve, 1)
                nc.vector.tensor_scalar(node_id[:], win[:], iota_p[:, 0:1], None, ALU.add).then_inc(pass_dve, 1)
                nc.vector.tensor_scalar(start[:], start[:], float(P), None, ALU.add).then_inc(pass_dve, 1)
                dve.wait_ge(pass_dve, steps + 4)
                dve.sem_inc(pass_go[layer], 1)

            def by_tile(ap):
                return ap.unsqueeze(2).to_broadcast([P, J, P])

            nodes(0)
            link(nc.vector.tensor_copy(start[:], base[:]))
            with dve.Fori(0, passes) as w:
                windows(0, w, 4 * w)
                with dve.Fori(0, GU) as i:
                    turn = dve.snap(w * GU + i)
                    for s in range(U):
                        q = U * turn + s
                        g = U * i + s
                        dve.wait_ge(bc0, q + w + 1)
                        nc.vector.tensor_scalar(to_edge[:, 0, :], bc_dst.rearrange("p b n -> p (b n)"),
                                                node_id[:, bass.ds(g, 1)], None, ALU.is_equal).then_inc(to_edge0, 1)
                        dve.wait_ge(idx_in[0][s], 16 * (turn + 1))
                        nc.vector.tensor_scalar(rel[:], idx[:, s, J:2 * J], win[:, bass.ds(g, 1)], None,
                                                ALU.subtract).then_inc(dve0, 1)
                        dve.wait_ge(dve0, STEPS0 * q + 1)
                        dve.wait_ge(acc_up, q + 1)
                        nc.vector.tensor_tensor(to_node[:, s % 2, :].rearrange("p (j n) -> p j n", j=J),
                                                iota_n[:].unsqueeze(1).to_broadcast([P, J, P]), by_tile(rel[:]),
                                                ALU.is_equal).then_inc(dve0, 1)
                        row = gat[:, s, 0:J * TW].rearrange("p (j f) -> p j f", j=J)
                        dve.wait_ge(expanded, q + 1)
                        dve.wait_ge(gathered[0][s], 16 * J * (turn + 1))
                        nc.vector.tensor_tensor(lin[:], ps[:, 6 + s % 2, 0:J * HEADS].rearrange(
                            "p (j h) -> p j h", j=J), row[:, :, F:TW], ALU.add).then_inc(dve0, 1)
                        dve.wait_ge(dve0, STEPS0 * q + 3)
                        nc.vector.scalar_tensor_tensor(att[:], lin[:], SLOPE, lin[:], ALU.mult,
                                                       ALU.max).then_inc(dve0, 1)
                        dve.wait_ge(dve0, STEPS0 * q + 4)
                        nc.vector.tensor_tensor(
                            msg[:, s % 2, :].rearrange("p (j h d) -> p j h d", j=J, h=HEADS),
                            row[:, :, 0:F].rearrange("p j (h d) -> p j h d", h=HEADS),
                            att[:].unsqueeze(3).to_broadcast([P, J, HEADS, HD]), ALU.mult).then_inc(msgs0, 1)

            nodes(1)
            link(nc.vector.tensor_copy(start[:], base[:]))

            def front(w, g, s, f, r):
                at = FRONT * f
                dve.wait_ge(bc1, 2 * f + 1)
                nc.vector.tensor_scalar(to_edge[:, s % 2, :], bc_dst.rearrange("p b n -> p (b n)"),
                                        node_id[:, bass.ds(g, 1)], None, ALU.is_equal).then_inc(to_edge1, 1)
                dve.wait_ge(idx_in[1][s], 16 * (r + 1))
                nc.vector.tensor_copy(srcf[:], idx[:, s, 0:J]).then_inc(dve1, 1)
                nc.vector.tensor_scalar(rel[:], idx[:, s, J:2 * J], win[:, bass.ds(g, 1)], None,
                                        ALU.subtract).then_inc(dve1, 1)
                dve.wait_ge(dve1, at + 1)
                dve.wait_ge(bc1, 2 * f + 2)
                nc.vector.tensor_tensor(same[:, s % 2, :].rearrange("p (j n) -> p j n", j=J),
                                        bc_src.rearrange("p b (t n) -> p (b t) n", t=4), by_tile(srcf[:]),
                                        ALU.is_equal).then_inc(same1, 1)
                dve.wait_ge(dve1, at + 2)
                nc.vector.tensor_scalar(above[:], rel[:], 0.0, None, ALU.is_ge).then_inc(dve1, 1)
                dve.wait_ge(dve1, at + 3)
                nc.vector.scalar_tensor_tensor(mask[:, s % 2, :], rel[:], float(P), above[:], ALU.is_lt,
                                               ALU.mult).then_inc(dve1, 1)
                dve.wait_ge(same1, f + 2)
                nc.vector.tensor_reduce(count[:], same[:, s % 2, :].rearrange("p (j n) -> p j n", j=J), AX.X,
                                        ALU.add).then_inc(dve1, 1)
                dve.wait_ge(dve1, at + 5)
                nc.vector.tensor_scalar(first[:], count[:], 1.0, None, ALU.is_equal).then_inc(dve1, 1)
                dve.wait_ge(dve1, at + 6)
                nc.vector.scalar_tensor_tensor(shift[:], srcf[:], dump[:, 0:1], first[:], ALU.subtract,
                                               ALU.mult).then_inc(dve1, 1)
                dve.wait_ge(dve1, at + 7)
                nc.vector.tensor_scalar(sidx[:, s, :], shift[:], dump[:, 0:1], None, ALU.add).then_inc(sidx_up, 1)

            with dve.Fori(0, passes) as w:
                windows(1, w, 4 * (passes + w))
                front(w, 0, 0, w * G + w, w * GU + w)
                with dve.Fori(0, GU) as i:
                    turn = dve.snap(w * GU + i)
                    for s in range(U):
                        q = U * turn + s
                        dve.wait_ge(gathered[1][s], 16 * J * ((turn + w + 1) if s == 0 else (turn + 1)))
                        for k in range(4):
                            dve.wait_ge(z_up, 4 * q + k + 1)
                            nc.vector.tensor_tensor(
                                pre[:, 2 * k:2 * k + 2, :],
                                ps[:, 4 + k % 2, :].rearrange("p (j f) -> p j f", j=2),
                                gat[:, s, 4 * k * F:4 * (k + 1) * F].rearrange("p (j f) -> p j f", j=2),
                                ALU.add).then_inc(pre_up, 1)
                        for h in range(2):
                            dve.wait_ge(acts, 2 * q + h + 1)
                            nc.vector.tensor_tensor(msg[:, 0, 512 * h:512 * (h + 1)],
                                                    pos[:, 4 * h:4 * h + 4, :].rearrange("p j f -> p (j f)"),
                                                    sig[:, 4 * h:4 * h + 4, :].rearrange("p j f -> p (j f)"),
                                                    ALU.mult).then_inc(m_up, 1)
                        nxt = (s + 1) % U
                        dve.wait_ge(sum_free, q + 1)
                        front(w, U * i + s + 1, nxt, q + w + 1, (turn + w + 1) if nxt == 0 else turn)

            for n in range(FIN):
                s = n % U
                dve.wait_ge(fin_in[s], 16 * K * (n // U + 1))
                nc.vector.tensor_tensor(gat[:, s, 0:FW], gat[:, s, 0:FW], gat[:, s, FW:2 * FW],
                                        ALU.add).then_inc(fin_dve, 1)
                dve.wait_ge(fin_dve, n + 1)
                dve.wait_ge(fin_pool, n + 1)
                nc.vector.tensor_tensor(gat[:, s, 0:FW], gat[:, s, 0:FW], gat[:, s, 2 * FW:3 * FW],
                                        ALU.add).then_inc(fin_sum, 1)


_INS = ["x", "src", "dst", "edge_attr_128", "L0_gnn_W", "L0_gnn_a", "L1_gnn_W_weight", "L1_gnn_b_weight",
        "L1_gnn_W_gate", "L1_gnn_b_gate"]


def kernel(**inputs):
    import numpy as _np
    import concourse.bacc as _bacc
    from concourse import mybir as _mybir
    from concourse.bass_utils import run_bass_kernel_spmd as _run

    nc = _bacc.Bacc("TRN2", target_bir_lowering=False, num_devices=1)
    arrays, args = {}, []
    for name in _INS:
        v = _np.ascontiguousarray(inputs[name])
        arrays[f"in_{name}"] = v
        args.append(nc.dram_tensor(f"in_{name}", v.shape, _mybir.dt.from_np(v.dtype), kind="ExternalInput").ap())
    shape = arrays["in_x"].shape
    args.append(nc.dram_tensor("out_x", shape, _mybir.dt.float32, kind="ExternalOutput").ap())
    gnn_kernel(nc, *args)
    r = _run(nc, [arrays], core_ids=[0])
    return r.results[0]["out_x"]
```
